# Optimizing a Trainium2 kernel written in Bass

```python
import numpy as np
import jax
import jax.numpy as jnp

def _softmax(x, axis=-1):
    return jax.nn.softmax(x, axis=axis)

def _gelu(x):
    return jax.nn.gelu(x, approximate=True)

def _silu(x):
    return jax.nn.silu(x)

def _sigmoid(x):
    return jax.nn.sigmoid(x)

def _layernorm(x, axis=-1, eps=1e-05):
    m = jnp.mean(x, axis=axis, keepdims=True)
    v = jnp.var(x, axis=axis, keepdims=True)
    return (x - m) / jnp.sqrt(v + eps)

def _scatter_add(tgt, idx, src, axis=0):
    return tgt.at[idx].add(src)

def _segment_sum(src, seg, n):
    return jax.ops.segment_sum(src, seg, n)
kernel_name = 'mk_conv_preact_d2_conv_nchw64_r2_18a9b7'

def setup_inputs(seed: int=0):
    np.random.seed(seed)
    _w = jnp.asarray

    def _rec_inputs():
        import jax
        import jax.numpy as jnp
        _gk = jax.random.key(seed)
        x = -0.000125 + 0.9999 * jax.random.normal(jax.random.fold_in(_gk, 1), (8, 32, 128, 128), jnp.float32)
        return x
    x = _rec_inputs()

    def _L0_conv_setup():
        import jax, jax.numpy as jnp
        import numpy as np
        from jax import lax
        DWT_SCALE = 0.5
        IDWT_SCALE = 1.0
        PAD = 2

        def haar_dwt(x, s):
            a = x[..., 0::2, 0::2]
            b = x[..., 0::2, 1::2]
            c = x[..., 1::2, 0::2]
            d = x[..., 1::2, 1::2]
            ll = s * (a + b + c + d)
            lh = s * (a + b - c - d)
            hl = s * (a - b + c - d)
            hh = s * (a - b - c + d)
            return (ll, lh, hl, hh)

        def haar_idwt(ll, lh, hl, hh, s):
            a = s * (ll + lh + hl + hh)
            b = s * (ll + lh - hl - hh)
            c = s * (ll - lh + hl - hh)
            d = s * (ll - lh - hl + hh)
            B, C, H2, W2 = ll.shape
            top = jnp.stack([a, b], axis=-1).reshape(B, C, H2, 2 * W2)
            bot = jnp.stack([c, d], axis=-1).reshape(B, C, H2, 2 * W2)
            return jnp.stack([top, bot], axis=-2).reshape(B, C, 2 * H2, 2 * W2)

        def conv2d(x, w, pad):
            return lax.conv_general_dilated(x, w, window_strides=(1, 1), padding=[(pad, pad), (pad, pad)], dimension_numbers=('NCHW', 'OIHW', 'NCHW'))
        key = jax.random.key(seed)
        kx, k0, k1, k2, kb = jax.random.split(key, 5)
        C, K = (32, 5)
        x = jax.random.normal(kx, (8, C, 128, 128), dtype=jnp.float32)
        scale = 0.02
        w0 = jax.random.normal(k0, (4 * C, 4 * C, K, K), dtype=jnp.float32) * scale
        w1 = jax.random.normal(k1, (4 * C, 4 * C, K, K), dtype=jnp.float32) * scale
        w2 = jax.random.normal(k2, (4 * C, 4 * C, K, K), dtype=jnp.float32) * scale
        bias = jax.random.normal(kb, (C,), dtype=jnp.float32) * 0.01
        return {'x': x, 'w0': w0, 'w1': w1, 'w2': w2, 'bias': bias}
    _L0_conv_all = _L0_conv_setup()
    _L0_conv_in = {k: v for k, v in _L0_conv_all.items() if k in ('w0', 'w1', 'w2', 'bias')}
    del _L0_conv_all

    def _L1_conv_setup():
        import jax, jax.numpy as jnp
        import numpy as np
        K = 5
        PAD = K // 2
        EPS = 1e-08

        def _extract_patches(x):
            B, C, H, W = x.shape
            xp = jnp.pad(x, ((0, 0), (0, 0), (PAD, PAD), (PAD, PAD)))
            taps = [xp[:, :, i:i + H, j:j + W] for i in range(K) for j in range(K)]
            return jnp.stack(taps, axis=2)
        key = jax.random.key(seed)
        k1, k2 = jax.random.split(key)
        x = jax.random.normal(k1, (8, 32, 56, 56), dtype=jnp.float32)
        spatial_weight = jax.random.normal(k2, (K * K,), dtype=jnp.float32)
        return {'x': x, 'spatial_weight': spatial_weight}
    _L1_conv_all = _L1_conv_setup()
    _L1_conv_in = {k: v for k, v in _L1_conv_all.items() if k in ('spatial_weight',)}
    del _L1_conv_all
    return {'x': x, 'L0_conv_w0': _L0_conv_in['w0'], 'L0_conv_w1': _L0_conv_in['w1'], 'L0_conv_w2': _L0_conv_in['w2'], 'L0_conv_bias': _L0_conv_in['bias'], 'L1_conv_spatial_weight': _L1_conv_in['spatial_weight']}

def reference(x, L0_conv_w0, L0_conv_w1, L0_conv_w2, L0_conv_bias, L1_conv_spatial_weight):
    import jax
    import jax.numpy as jnp

    def _L0_conv_ref(x, w0, w1, w2, bias):
        import jax, jax.numpy as jnp
        import numpy as np
        from jax import lax
        DWT_SCALE = 0.5
        IDWT_SCALE = 1.0
        PAD = 2

        def haar_dwt(x, s):
            a = x[..., 0::2, 0::2]
            b = x[..., 0::2, 1::2]
            c = x[..., 1::2, 0::2]
            d = x[..., 1::2, 1::2]
            ll = s * (a + b + c + d)
            lh = s * (a + b - c - d)
            hl = s * (a - b + c - d)
            hh = s * (a - b - c + d)
            return (ll, lh, hl, hh)

        def haar_idwt(ll, lh, hl, hh, s):
            a = s * (ll + lh + hl + hh)
            b = s * (ll + lh - hl - hh)
            c = s * (ll - lh + hl - hh)
            d = s * (ll - lh - hl + hh)
            B, C, H2, W2 = ll.shape
            top = jnp.stack([a, b], axis=-1).reshape(B, C, H2, 2 * W2)
            bot = jnp.stack([c, d], axis=-1).reshape(B, C, H2, 2 * W2)
            return jnp.stack([top, bot], axis=-2).reshape(B, C, 2 * H2, 2 * W2)

        def conv2d(x, w, pad):
            return lax.conv_general_dilated(x, w, window_strides=(1, 1), padding=[(pad, pad), (pad, pad)], dimension_numbers=('NCHW', 'OIHW', 'NCHW'))
        weights = [w0, w1, w2]
        idwt_s = DWT_SCALE * IDWT_SCALE
        curr = x
        ll_levels, high_levels = ([], [])
        for w in weights:
            ll, lh, hl, hh = haar_dwt(curr, DWT_SCALE)
            curr = ll
            B, C, H2, W2 = ll.shape
            stacked = jnp.stack([ll, lh, hl, hh], axis=2).reshape(B, 4 * C, H2, W2)
            y = conv2d(stacked, w, PAD)
            y = y.reshape(B, -1, 4, H2, W2)
            ll_levels.append(y[:, :, 0])
            high_levels.append(y[:, :, 1:])
        next_ll = jnp.zeros_like(ll_levels[-1])
        for ll_t, h_t in zip(reversed(ll_levels), reversed(high_levels)):
            ll = ll_t + next_ll
            next_ll = haar_idwt(ll, h_t[:, :, 0], h_t[:, :, 1], h_t[:, :, 2], idwt_s)
        return next_ll + bias.reshape(1, -1, 1, 1)

    def _L1_conv_ref(x, spatial_weight):
        import jax, jax.numpy as jnp
        import numpy as np
        K = 5
        PAD = K // 2
        EPS = 1e-08

        def _extract_patches(x):
            B, C, H, W = x.shape
            xp = jnp.pad(x, ((0, 0), (0, 0), (PAD, PAD), (PAD, PAD)))
            taps = [xp[:, :, i:i + H, j:j + W] for i in range(K) for j in range(K)]
            return jnp.stack(taps, axis=2)
        patches = _extract_patches(x)
        dot = jnp.einsum('bchw,bckhw->bkhw', x, patches)
        norm_x = jnp.sqrt(jnp.sum(x * x, axis=1))
        norm_p = jnp.sqrt(jnp.sum(patches * patches, axis=1))
        sim = dot / jnp.maximum(norm_x[:, None] * norm_p, EPS)
        likelihood = (sim + 1.0) * 0.5
        weight = likelihood * spatial_weight[None, :, None, None]
        out = jnp.einsum('bckhw,bkhw->bchw', patches, weight)
        return out

    def _gn(v, G=32, eps=1e-05):
        B_, C_, H_, W_ = v.shape
        g = v.reshape(B_, G, C_ // G, H_, W_)
        m = jnp.mean(g, axis=(2, 3, 4), keepdims=True)
        s = jnp.var(g, axis=(2, 3, 4), keepdims=True)
        return ((g - m) / jnp.sqrt(s + eps)).reshape(v.shape)

    def _ln_c(v, eps=1e-06):
        m = jnp.mean(v, axis=1, keepdims=True)
        s = jnp.var(v, axis=1, keepdims=True)
        return (v - m) / jnp.sqrt(s + eps)

    def _ln_t(v, eps=1e-05):
        m = jnp.mean(v, axis=-1, keepdims=True)
        s = jnp.var(v, axis=-1, keepdims=True)
        return (v - m) / jnp.sqrt(s + eps)

    def _to_tokens(v):
        B_, C_, H_, W_ = v.shape
        return v.reshape(B_, C_, H_ * W_).transpose(0, 2, 1)

    def _from_tokens(t, like):
        B_, C_, H_, W_ = like.shape
        return t.transpose(0, 2, 1).reshape(B_, C_, H_, W_)
    x = x + _L0_conv_ref(_gn(x), L0_conv_w0, L0_conv_w1, L0_conv_w2, L0_conv_bias)
    x = x + _L1_conv_ref(_gn(x), L1_conv_spatial_weight)
    return x

_drawn_inputs = setup_inputs


def setup_inputs(seed=0):
    import zlib

    import numpy as np

    out = dict(_drawn_inputs(seed))
    spreads = {}
    factors = {'L0_conv_bias': 8.0}
    for name, (base, spread) in spreads.items():
        noise = np.random.default_rng([zlib.crc32(name.encode()), seed]).standard_normal(out[name].shape)
        drawn = base * np.exp(spread * noise) if base else spread * noise
        out[name] = jnp.asarray(drawn.astype(out[name].dtype))
    for name, factor in factors.items():
        out[name] = (out[name] * factor).astype(out[name].dtype)
    return out
```

```python
from contextlib import ExitStack

import numpy as np

import concourse.bass as bass
from concourse import mybir

F32 = mybir.dt.float32
F16 = mybir.dt.float16
I32 = mybir.dt.int32
ALU = mybir.AluOpType
ACT = mybir.ActivationFunctionType
AX_X = mybir.AxisListType.X

P = 128
C = 32
Q = 4
B = 8
IMG = 128
H0, H1, H2 = IMG // 2, IMG // 4, IMG // 8
K = 5
TAPS = K * K
BANK = 512
CONV_TILES = H0 * H0 // BANK
CROWS = H0 // CONV_TILES
CHUNK = 16
CHUNKS = H0 // CHUNK
X_SCALE = 32.0
SIM_SCALE = 64.0
EPS_GN = 1e-5
EPS_SIM = 1e-8

TH, TW = 4, 8
QN = Q * TH * TW
KH, KW = TH + 2, TW + 2
KQ = KH * KW
KN = 64 + KQ
BANDS = 4
BH, UW = H0 // BANDS, H0 // 2
SH = BH + 2
STRIPS = H0 // TW
SN = SH * KW
GROUPS = UW // TW
UN = GROUPS * SN
PIECE = UN // 2
UNITS = 2 * BANDS
PAIRS = 2 * GROUPS
START = 1
HOOKS = [8 * n for n in range(9)]

PAD_EDGE = P * (2 * SH + STRIPS * KW - 2)
PAD_INNER = P * 2 * SH

GN_LINKS = 6
PREP_LINKS = 7


def host_constants():
    haar = np.array([[1, 1, 1, 1], [1, 1, -1, -1], [1, -1, 1, -1], [1, -1, -1, 1]], np.float32)
    mix = np.zeros((P, P), np.float32)
    gather = np.zeros((P, Q, P), np.float16)
    for c in range(C):
        for t in range(Q):
            for q in range(Q):
                mix[4 * c + t, C * q + c] = 0.5 * haar[t, q]
                gather[C * q + c, t, C * t + c] = 0.5
    part = np.arange(P)
    average = np.where(part[:, None] % C == part[None] % C, 0.25, 0).astype(np.float32)
    same_quadrant = (part[:, None] // C == part[None] // C).astype(np.float32)
    square = np.stack([mix, average, same_quadrant, np.eye(P, dtype=np.float32)], 1)
    unpair = np.zeros((2 * C, C), np.float16)
    unpair[np.arange(2 * C), np.arange(2 * C) % C] = 1 / X_SCALE
    q, h, w = np.meshgrid(np.arange(Q), np.arange(TH), np.arange(TW), indexing="ij")
    qr, qc = (2 * h + q // 2).ravel(), (2 * w + q % 2).ravel()
    taps = np.zeros((KN, TAPS, 2, QN), np.float16)
    h, w = np.meshgrid(np.arange(KH), np.arange(KW), indexing="ij")
    for k in range(Q):
        dr = (2 * (h - 1) + k // 2).reshape(-1, 1) - qr[None]
        dc = (2 * (w - 1) + k % 2).reshape(-1, 1) - qc[None]
        for t in range(TAPS):
            taps[64 * (k % 2):64 * (k % 2) + KQ, t, k // 2] = (dr == t // K - K // 2) & (dc == t % K - K // 2)
    return square, gather, taps.reshape(KN, TAPS * 2 * QN), unpair


def first(n):
    return isinstance(n, int) and n == 0


class Chain:

    def __init__(self, sem, per_round):
        self.sem, self.per_round, self.base, self.k = sem, per_round, 0, 0

    def round(self, n):
        self.base, self.k = n * self.per_round, 0

    def link(self, engine, instruction):
        self.k += 1
        assert self.k <= self.per_round
        instruction.then_inc(self.sem, 1)
        engine.wait_ge(self.sem, self.base + self.k)


def build(nc, x, w0, w1, w2, bias, spatial, square, gather, tapmask, unpair, out):
    ctx = ExitStack()
    with ctx:
        def sb(name, shape, dt):
            return ctx.enter_context(nc.sbuf_tensor(name, shape, dt))

        def psum(name):
            return ctx.enter_context(nc.psum_tensor(name, [P, BANK], F32))

        def sem(name):
            return ctx.enter_context(nc.semaphore(name))

        wconv = sb("wconv", [P, 3, 2, TAPS, P], F16)
        xh, xl = sb("xh", [P, H0, H0], F16), sb("xl", [P, H0, H0], F16)
        xh1, xl1 = sb("xh1", [P, H1, H1], F16), sb("xl1", [P, H1, H1], F16)
        xh2, xl2 = sb("xh2", [P, H2, H2], F16), sb("xl2", [P, H2, H2], F16)
        ring = sb("ring", [P, 2, CHUNK * IMG], F32)
        xacc = sb("xacc", [P, H0, H0], F32)
        x1 = sb("x1", [P, H0, H0], F32)
        unit_mem = sb("unit_mem", [P, 2, 3 * Q * UN], F16)
        x1_res = sb("x1_res", [P, Q, TH, H0], F32)
        st_x2 = sb("st_x2", [P, STRIPS, SH, KW], F32)
        st_v = sb("st_v", [P, 2, 2, UN], F16)
        st_hl = sb("st_hl", [P, 2, 2, UN], F16)
        st_n = sb("st_n", [P, 2, UN], F32)
        st_a, st_b = sb("st_a", [P, UN], F32), sb("st_b", [P, UN], F32)
        wgt = sb("wgt", [KN, 2, BANDS, 2 * QN], F32)
        vals = sb("vals", [KN, 2 * BANDS * GROUPS, C], F32)
        ostage = sb("ostage", [P, 2 * TH, IMG], F32)
        z2 = sb("z2", [P, H2 * H2], F32)
        z1 = sb("z1", [P, H1, H1], F32)
        up = sb("up", [P, 2, H1 * H1], F32)
        tapw = sb("tapw", [KN, 2 * QN], F32)
        sq_c = sb("sq_c", [P, 4, P], F32)
        gat_c = sb("gat_c", [P, Q, P], F16)
        unpair_c = sb("unpair_c", [2 * C, C], F16)
        bn1, bn2 = sb("bn1", [P, CONV_TILES, 6], F32), sb("bn2", [P, CONV_TILES, 6], F32)
        gn1, gn2 = sb("gn1", [P, 10], F32), sb("gn2", [P, 10], F32)
        small = sb("small", [P, 16], F32)
        spat = sb("spat", [P, TAPS], F32)
        short = sb("short", [P, 2], F32)
        flag = sb("flag", [1, 1], I32)
        ones = sb("ones", [P, 1], F32)
        mix, average, same_quadrant, ident = (sq_c[:, n, :] for n in range(4))
        unscale = [small[:, n:n + 1] for n in range(3)]
        wscale = [small[:, 3 + n:4 + n] for n in range(3)]
        biasq = small[:, 6:7]
        ones_row = sq_c[0:1, 2, 0:C]

        def unit_part(s, n):
            return unit_mem[:, s, n * Q * UN:(n + 1) * Q * UN].rearrange("p (q e n) -> p q e n", q=Q, e=GROUPS)

        keys, queries, values = ([unit_part(s, n) for s in range(2)] for n in range(3))
        norm_rows = [unit_mem[:, s, 2 * Q * UN:3 * Q * UN].bitcast(F32).rearrange("p (q e n) -> p q e n", q=Q, e=2)
                     for s in range(2)]
        wraw = [unit_mem[:, 0, 0:2 * TAPS * P].bitcast(F32), unit_mem[:, 1, 0:2 * TAPS * P].bitcast(F32), x1[:, :, :].rearrange("p a b -> p (a b)")[:, 0:TAPS * P]]
        wmix = xacc[:, :, :].rearrange("p a b -> p (a b)")[:, 0:TAPS * P]
        tap_c = ring[:, :, :].rearrange("p a b -> p (a b)")[0:KN, 0:TAPS * QN].bitcast(F16)

        conv_ps = [psum("conv0"), psum("conv1")]
        gram_ps = [psum("gram0"), psum("gram1")]
        vals_ps, out_ps, guard_ps, stat_ps = psum("vals_ps"), psum("out_ps"), psum("guard_ps"), psum("stat_ps")

        def dram(name, shape, dt):
            return nc.dram_tensor(name, shape, dt, kind="Internal").ap()

        d_z2, d_z1 = dram("d_z2", [B, P, H2 * H2], F32), dram("d_z1", [B, P, H1 * H1], F32)
        d_x1 = dram("d_x1", [B, P, H0 * H0], F32)
        d_hl = dram("d_hl", [B, BANDS, P, 2, 2, UN], F16)
        d_v = dram("d_v", [B, BANDS, P, 2, 2, UN], F16)
        d_n = dram("d_n", [B, BANDS, Q, 2, UN], F32)

        passed = sem("passed")
        const_in = sem("const_in")
        wraw_in = [sem(f"wraw_in{n}") for n in range(3)]
        wmixed = sem("wmixed")
        wmix_kept = sem("wmix_kept")
        wlevel = sem("wlevel")
        wlevel_mm = sem("wlevel_mm")
        wfull = sem("wfull")
        whigh = sem("whigh")
        wlow = sem("wlow")
        setup = sem("setup")
        zeroed = sem("zeroed")
        tapw_done = sem("tapw_done")
        raw_in = [sem("raw_in0"), sem("raw_in1")]
        bn1_done = sem("bn1_done")
        gn1_part, gn2_part = sem("gn1_part"), sem("gn2_part")
        gn1_mm, gn2_mm = sem("gn1_mm"), sem("gn2_mm")
        gn1_var, gn2_var = sem("gn1_var"), sem("gn2_var")
        gn1_root, gn2_root = sem("gn1_root"), sem("gn2_root")
        gn1_link, gn2_link = sem("gn1_link"), sem("gn2_link")
        gn1_done, gn2_done = sem("gn1_done"), sem("gn2_done")
        high_done = sem("high_done")
        acc_done = sem("acc_done")
        rest_done = sem("rest_done")
        low_done = sem("low_done")
        ll_ready = sem("ll_ready")
        ll_high = sem("ll_high")
        ll_low = sem("ll_low")
        conv_ready = sem("conv_ready")
        z2_done = sem("z2_done")
        z2_saved, z1_saved = sem("z2_saved"), sem("z1_saved")
        up2_in = sem("up2_in")
        u2_done = sem("u2_done")
        z1_done = sem("z1_done")
        up_in = [sem("up_in0"), sem("up_in1")]
        up_added = sem("up_added")
        x1_done = sem("x1_done")
        x1_saved = [sem(f"x1_saved{r}") for r in range(BANDS)]
        bn2_done = sem("bn2_done")
        pad_zero = sem("pad_zero")
        x2_done = sem("x2_done")
        sq_done = sem("sq_done")
        v_high = sem("v_high")
        n2_ready = sem("n2_ready")
        n2_root = sem("n2_root")
        n2_kept = sem("n2_kept")
        prep_link = sem("prep_link")
        unit_vec = sem("unit_vec")
        unit_high = sem("unit_high")
        unit_low = sem("unit_low")
        count_ready = sem("count_ready")
        flag_done = sem("flag_done")
        band_saved = sem("band_saved")
        unit_in = [sem("unit_in0"), sem("unit_in1")]
        x1_res_in = sem("x1_res_in")
        vt_ready = sem("vt_ready")
        vals_done = sem("vals_done")
        gram_ready = sem("gram_ready")
        wgt_done = sem("wgt_done")
        group_done = sem("group_done")
        unit_out = sem("unit_out")
        half_out = sem("half_out")
        stored = sem("stored")

        def alone(engine):
            engine.sem_inc(passed, 1)

        block = ctx.enter_context(nc.Block())

        @block.sync
        def _(sp):
            sp.sem_inc(band_saved, START)
            sp.sem_inc(stored, START)
            sp.dma_start(sq_c[:, :, :], square).then_inc(const_in, 16)
            for n, w in enumerate((w0, w1, w2)):
                sp.dma_start(wraw[n], w.rearrange("o i a b -> o (i a b)")).then_inc(wraw_in[n], 16)
            sp.dma_start(gat_c[:, :, :], gather).then_inc(const_in, 16)
            for q in range(Q):
                sp.dma_start(small[C * q:C * q + C, 6:7], bias.rearrange("(c a) -> c a", a=1)).then_inc(const_in, 16)
            sp.dma_start(spat[:, :], spatial.rearrange("(a k) -> a k", a=1).to_broadcast([P, TAPS])).then_inc(const_in, 16)
            sp.dma_start(tap_c, tapmask).then_inc(const_in, 16)
            sp.dma_start(unpair_c[:, :], unpair).then_inc(const_in, 16)

            def save_band(b, r):
                sp.wait_ge(unit_low, 8 * b + 2 * r + 2)
                sp.dma_start(d_hl[b, r], st_hl[:, :, :, :]).then_inc(band_saved, 16)
                sp.dma_start(d_v[b, r], st_v[:, :, :, :]).then_inc(band_saved, 16)
                sp.dma_start(d_n[b, r], st_n[0:P:C, :, :]).then_inc(band_saved, 16)

            def load_unit(b, u):
                r, half, s = u // 2, u % 2, u % 2
                sp.wait_ge(band_saved, START + 48 * (4 * b + r + 1))
                alone(sp)
                if u >= 2:
                    sp.wait_ge(group_done, START + 4 * (8 * b + u - 1))
                else:
                    sp.wait_ge(group_done, START + 32 * b)
                for dst, order in ((keys[s], (0, 1, 0, 1)), (queries[s], (0, 0, 1, 1))):
                    for j, hl in enumerate(order):
                        sp.dma_start(dst[C * j:C * j + C].rearrange("c q e n -> c q (e n)"),
                                     d_hl[b, r, :, hl, half, :].rearrange("(q c) n -> c q n", c=C)).then_inc(unit_in[s], 16)
                for hl in range(2):
                    sp.dma_start(values[s][C * hl:C * hl + C].rearrange("c q e n -> c q (e n)"),
                                 d_v[b, r, :, hl, half, :].rearrange("(q c) n -> c q n", c=C)).then_inc(unit_in[s], 16)
                for g in range(2):
                    sp.dma_start(norm_rows[s][64 + C * g:65 + C * g].rearrange("a q e n -> a q (e n)"),
                                 d_n[b, r, :, half, UN // 2 * g:UN // 2 * (g + 1)].rearrange("(a q) n -> a q n", a=1))\
                        .then_inc(unit_in[s], 16)

            def load_residual(b, r):
                sp.wait_ge(x1_saved[r], 16 * b + 16)
                alone(sp)
                sp.wait_ge(unit_out, START + 8 * b + 2 * r)
                src = d_x1[b].rearrange("(q c) (h w) -> c q h w", c=C, w=H0)
                for g in range(BANDS):
                    row = BH * r + TH * g
                    sp.dma_start(x1_res[C * g:C * g + C].rearrange("c q h w -> c q (h w)"),
                                 src[:, :, row:row + TH, :].rearrange("c q h w -> c q (h w)")).then_inc(x1_res_in, 16)

            def store_band(b, r):
                sp.wait_ge(unit_out, START + 8 * b + 2 * r + 2)
                for g in range(BANDS):
                    row = 2 * (BH * r + TH * g)
                    sp.dma_start(out[b, :, row:row + 2 * TH, :].rearrange("c h w -> c (h w)"),
                                 ostage[C * g:C * g + C].rearrange("c h w -> c (h w)")).then_inc(stored, 16)

            def iteration(b):
                save_band(b, 0)
                load_unit(b, 0)
                load_unit(b, 1)
                load_residual(b, 0)
                save_band(b, 1)
                for r in range(BANDS):
                    if r + 1 < BANDS:
                        if r + 1 >= 2:
                            save_band(b, r + 1)
                        load_unit(b, 2 * r + 2)
                        load_unit(b, 2 * r + 3)
                    store_band(b, r)
                    if r + 1 < BANDS:
                        load_residual(b, r + 1)

            with sp.Fori(1, B + 1) as i:
                iteration(i - 1)
            sp.wait_ge(stored, START + 4 * 64 * B)

        @block.gpsimd
        def _(pool):
            nc.gpsimd.memset(ones[:, :], 1.0).then_inc(zeroed, 1)
            nc.gpsimd.memset(st_x2[:, :, :, :], 0.0).then_inc(zeroed, 1)

            def load_raw(batch, c, slot):
                alone(pool)
                for q in range(Q):
                    cp = q % 2
                    src = x[batch].rearrange("c (h a) w -> c a h w", a=2)[:, q // 2, CHUNK * c:CHUNK * (c + 1), cp:IMG]
                    dst = ring[C * q:C * q + C, slot, :].rearrange("p (h w) -> p h w", w=IMG)[:, :, 0:IMG - cp]
                    pool.dma_start(dst, src).then_inc(raw_in[slot], 16)

            def raw_for_stats(n, batch, cs):
                for c in cs:
                    if c >= 2:
                        pool.wait_ge(bn1_done, 4 * n + c - 1)
                    elif not first(n):
                        pool.wait_ge(low_done, 4 * (n - 1) + 3 + c)
                    load_raw(batch, c, c % 2)

            def raw_for_split(n, batch, cs):
                for c in cs:
                    if c < 2:
                        pool.wait_ge(bn1_done, 4 * n + 3 + c)
                    else:
                        pool.wait_ge(low_done, 4 * n + c - 1)
                    load_raw(batch, c, c % 2)

            def iteration(i, nxt, conv, ls):
                b = i - 1
                if ls:
                    pool.wait_ge(x1_done, 8 * b + 8)
                    pool.dma_start(d_x1[b, :, 3 * BH * H0:], x1[:, 3 * BH:, :].rearrange("p h w -> p (h w)")).then_inc(x1_saved[3], 16)
                    pool.wait_ge(band_saved, START + 4 * 48 * b)
                    alone(pool)
                    nc.gpsimd.memset(st_x2[:, :, 0, :], 0.0).then_inc(pad_zero, 1)
                if conv:
                    raw_for_stats(i + 1, nxt, (0, 1))
                    pool.wait_ge(z2_done, i + 1)
                    pool.dma_start(d_z2[i], z2[:, :]).then_inc(z2_saved, 16)
                    pool.wait_ge(z2_saved, 16 * i + 16)
                    if not first(i):
                        pool.wait_ge(up_added, 4 * i)
                    alone(pool)
                    for q in range(Q):
                        pool.dma_start(up[C * q:C * q + C, 0, :].rearrange("c (q n) -> c q n", q=Q),
                                       d_z2[i].rearrange("(q c) n -> c q n", c=C)).then_inc(up2_in, 16)
                    raw_for_stats(i + 1, nxt, (2, 3))
                    pool.wait_ge(z1_done, 2 * i + 2)
                    pool.dma_start(d_z1[i], z1[:, :, :].rearrange("p h w -> p (h w)")).then_inc(z1_saved, 16)
                    pool.wait_ge(z1_saved, 16 * i + 16)
                    for q1 in range(Q):
                        if q1 >= 2:
                            pool.wait_ge(up_added, 4 * i + q1 - 1)
                        elif q1 == 0:
                            pool.wait_ge(u2_done, i + 1)
                        alone(pool)
                        for q in range(Q):
                            pool.dma_start(up[C * q:C * q + C, q1 % 2, :], d_z1[i, C * q1:C * q1 + C, :])\
                                .then_inc(up_in[q1 % 2], 16)
                    raw_for_split(i + 1, nxt, (0, 1))
                    for r in range(BANDS - 1):
                        pool.wait_ge(x1_done, 8 * i + 2 * r + 2)
                        pool.dma_start(d_x1[i, :, r * BH * H0:(r + 1) * BH * H0],
                                       x1[:, r * BH:(r + 1) * BH, :].rearrange("p h w -> p (h w)")).then_inc(x1_saved[r], 16)
                        if r == 0 and ls:
                            pool.wait_ge(band_saved, START + 48 * (4 * b + 3))
                            alone(pool)
                            nc.gpsimd.memset(st_x2[:, :, SH - 1, :], 0.0).then_inc(pad_zero, 1)
                        if r == 1:
                            raw_for_split(i + 1, nxt, (2,))
                    raw_for_split(i + 1, nxt, (3,))
                elif ls:
                    pool.wait_ge(band_saved, START + 48 * (4 * b + 3))
                    alone(pool)
                    nc.gpsimd.memset(st_x2[:, :, SH - 1, :], 0.0).then_inc(pad_zero, 1)

            pool.wait_ge(tapw_done, 1)
            raw_for_stats(0, 0, range(CHUNKS))
            raw_for_split(0, 0, range(CHUNKS))
            iteration(0, 1, True, False)
            with pool.Fori(1, B - 1) as i:
                iteration(i, i + 1, True, True)
            iteration(B - 1, 0, True, True)
            iteration(B, 0, False, True)
            pool.wait_ge(z2_saved, 16 * B)
            pool.wait_ge(z1_saved, 16 * B)
            for saved in x1_saved:
                pool.wait_ge(saved, 16 * B)
            pool.wait_ge(band_saved, START + 4 * 48 * B)

        @block.scalar
        def _(act):
            def copy(dst, src, scale=1.0, bias=0.0, func=ACT.Identity):
                return nc.scalar.activation(dst, src, func, bias=bias, scale=scale)

            act.sem_inc(unit_high, START)
            act.sem_inc(vals_done, START)
            act.wait_ge(const_in, 16 * 9)
            act.wait_ge(zeroed, 2)
            for n in range(3):
                for t in range(0, TAPS, 4):
                    m = min(4, TAPS - t)
                    k = 7 * n + t // 4
                    act.wait_ge(wmixed, k + 1)
                    if n > 0 and t == 0:
                        act.wait_ge(wfull, 7 * n)
                    copy(wmix[:, t * P:(t + m) * P], conv_ps[k % 2][:, 0:m * P]).then_inc(wmix_kept, 1)
                act.wait_ge(wlevel, 3 * n + 3)
                for t in range(0, TAPS, 4):
                    m = min(4, TAPS - t)
                    k = 7 * n + t // 4
                    act.wait_ge(wfull, k + 1)
                    copy(wconv[:, n, 0, t:t + m, :].rearrange("p t o -> p (t o)"), gram_ps[k % 2][:, 0:m * P],
                         scale=wscale[n]).then_inc(whigh, 1)

            def raw_chunk(c, slot):
                return ring[:, slot, 0:CHUNK * IMG:2]

            def rows(t, c):
                return t[:, CHUNK * c:CHUNK * (c + 1), :].rearrange("p h w -> p (h w)")

            def split_chunk(n, c):
                s = c % 2
                act.wait_ge(gn1_done, n + 1)
                act.wait_ge(raw_in[s], 64 * (4 * n + 3 + c // 2))
                if not first(n):
                    act.wait_ge(conv_ready, 11 * (n - 1) + 3 + min(2 * c + 3, CONV_TILES))
                    act.wait_ge(x1_done, 8 * (n - 1) + 2 * c + 2)
                copy(rows(xh, c), raw_chunk(c, s), scale=gn1[:, 8:9], bias=gn1[:, 9:10]).then_inc(high_done, 1)
                copy(rows(xacc, c), raw_chunk(c, s), bias=biasq).then_inc(acc_done, 1)

            def split_low(n, c):
                act.wait_ge(rest_done, 4 * n + c + 1)
                copy(rows(xl, c), raw_chunk(c, c % 2), bias=gn1[:, 9:10]).then_inc(low_done, 1)

            def root(g, var, done, n):
                act.wait_ge(var, n + 1)
                copy(g[:, 5:6], g[:, 4:5], func=ACT.Sqrt).then_inc(done, 1)

            def ll_highs(i, k):
                act.wait_ge(ll_ready, 3 * i + k + 1)
                if k < 2:
                    copy(xh1[:, 16 * k:16 * k + 16, :].rearrange("p h w -> p (h w)"), conv_ps[k][:, :]).then_inc(ll_high, 1)
                else:
                    copy(xh2[:, :, :].rearrange("p h w -> p (h w)"), conv_ps[0][:, 0:H2 * H2]).then_inc(ll_high, 1)

            def band_in(b, r):
                act.wait_ge(gn2_done, b + 1)
                if r == 0:
                    act.wait_ge(pad_zero, 2 * b + 1)
                    act.wait_ge(band_saved, START + 48 * 4 * b)
                else:
                    act.wait_ge(band_saved, START + 48 * (4 * b + r))
                    if r == BANDS - 1:
                        act.wait_ge(pad_zero, 2 * b + 2)
                lo, hi = max(BH * r - 1, 0), min(BH * r + BH + 1, H0)
                d = lo - (BH * r - 1)
                for e0, e1 in ((0, 1), (1, STRIPS - 1), (STRIPS - 1, STRIPS)):
                    c0, c1 = max(TW * e0 - 1, 0), min(TW * e0 + TW + 1, H0)
                    dc = c0 - (TW * e0 - 1)
                    src = x1[:, lo:hi, c0:c1]
                    src = bass.AP(src.tensor, src.offset, [src.ap[0], [TW, e1 - e0], src.ap[1], src.ap[2]])
                    last = copy(st_x2[:, e0:e1, d:d + hi - lo, dc:dc + c1 - c0], src, scale=gn2[:, 8:9], bias=gn2[:, 9:10])
                last.then_inc(x2_done, 1)
                act.wait_ge(x2_done, 4 * b + r + 1)
                for half in range(2):
                    part = st_x2[:, GROUPS * half:GROUPS * (half + 1), :, :].rearrange("p e h w -> p (e h w)")
                    copy(st_n[:, half, :], part, func=ACT.Square).then_inc(sq_done, 1)
                for half in range(2):
                    part = st_x2[:, GROUPS * half:GROUPS * (half + 1), :, :].rearrange("p e h w -> p (e h w)")
                    copy(st_v[:, 0, half, :], part, scale=X_SCALE).then_inc(v_high, 1)

            def norms(b, r, half):
                for p in range(2):
                    k = 4 * r + 2 * half + p
                    act.wait_ge(n2_ready, 16 * b + k + 1)
                    if p == 0:
                        act.wait_ge(unit_vec, START + 8 * b + 2 * r + half)
                    copy(st_a[:, p * PIECE:(p + 1) * PIECE], stat_ps[:, 0:PIECE], func=ACT.Sqrt).then_inc(n2_root, 1)
                    copy(st_n[:, half, p * PIECE:(p + 1) * PIECE], stat_ps[:, 0:PIECE]).then_inc(n2_kept, 1)

            def unit_highs(b, r, half):
                act.wait_ge(unit_vec, START + 8 * b + 2 * r + half + 1)
                copy(st_hl[:, 0, half, :], st_b[:, :]).then_inc(unit_high, 1)

            def vals_out(b, u, part):
                act.wait_ge(vt_ready, 16 * b + 2 * u + part + 1)
                act.wait_ge(group_done, START + 4 * (8 * b + u))
                copy(vals[:, 16 * part:16 * part + 16, :].rearrange("p n c -> p (n c)"), vals_ps[0:KN, :]).then_inc(vals_done, 1)

            def band_rest(b, r, half):
                norms(b, r, half)
                unit_highs(b, r, half)

            def iteration(i, conv, ls):
                b = i - 1
                if conv:
                    split_chunk(i, 3)
                    split_low(i, 3)
                    ll_highs(i, 0)
                    ll_highs(i, 1)
                    ll_highs(i, 2)
                if ls:
                    root(gn2, gn2_var, gn2_root, b)
                    band_in(b, 0)
                if conv:
                    act.wait_ge(conv_ready, 11 * i + 1)
                    if not first(i):
                        act.wait_ge(z2_saved, 16 * i)
                    copy(z2[:, :], conv_ps[1][:, 0:H2 * H2], scale=unscale[2]).then_inc(z2_done, 1)
                if ls:
                    band_rest(b, 0, 0)
                    band_rest(b, 0, 1)
                if conv:
                    act.wait_ge(up2_in, 64 * i + 64)
                    if not first(i):
                        act.wait_ge(z1_saved, 16 * i)
                    for q in range(Q):
                        last = copy(z1[:, q // 2:H1:2, q % 2:H1:2],
                                    up[:, 0, q * H2 * H2:(q + 1) * H2 * H2].rearrange("p (h w) -> p h w", w=H2), scale=0.5)
                    last.then_inc(u2_done, 1)
                if ls:
                    band_in(b, 1)
                for j in range(CONV_TILES):
                    if ls:
                        vals_out(b, j, 0)
                        if j in (0, 2, 4):
                            band_rest(b, 1 + j // 2, 0)
                        vals_out(b, j, 1)
                        if j in (0, 2, 4):
                            band_rest(b, 1 + j // 2, 1)
                        if j in (1, 3):
                            band_in(b, 2 + j // 2)
                    if conv:
                        if j == 1:
                            root(gn1, gn1_var, gn1_root, i + 1)
                        if j in (3, 5, 7):
                            split_chunk(i + 1, j // 2 - 1)
                            split_low(i + 1, j // 2 - 1)

            root(gn1, gn1_var, gn1_root, 0)
            for c in range(CHUNKS - 1):
                split_chunk(0, c)
                split_low(0, c)
            iteration(0, True, False)
            with act.Fori(1, B) as i:
                iteration(i, True, True)
            iteration(B, False, True)

        @block.vector
        def _(dve):
            V = nc.vector
            steps = Chain(setup, 200)
            for done in (unit_out, unit_vec, flag_done, wgt_done):
                dve.sem_inc(done, START)
            V.memset(vals_ps[:, :], 0.0)
            V.memset(guard_ps[:, :], 0.0)

            dve.wait_ge(const_in, 16 * 9)
            steps.link(dve, V.memset(tapw[:, :], 0.0))
            for t in range(TAPS):
                steps.link(dve, V.scalar_tensor_tensor(out=tapw[:, :], in0=tap_c[:, t * 2 * QN:(t + 1) * 2 * QN],
                                                       scalar=spat[0:KN, t:t + 1], in1=tapw[:, :],
                                                       op0=ALU.mult, op1=ALU.add))
            V.tensor_scalar(tapw[:, :], tapw[:, :], 0.5 / SIM_SCALE ** 2, None, ALU.mult).then_inc(tapw_done, 1)

            for n in range(3):
                a = gn1[:, 0:4]
                dve.wait_ge(wmix_kept, 7 * n + 7)
                V.tensor_reduce(out=a[:, 0:1], in_=wmix, op=ALU.max, axis=AX_X)
                steps.link(dve, V.tensor_reduce(out=a[:, 1:2], in_=wmix, op=ALU.min, axis=AX_X))
                steps.link(dve, V.tensor_scalar(a[:, 1:2], a[:, 1:2], -1.0, 1e-30, ALU.mult, ALU.max))
                V.tensor_tensor(a[:, 2:3], a[:, 0:1], a[:, 1:2], ALU.max).then_inc(wlevel, 1)
                dve.wait_ge(wlevel_mm, 2 * n + 1)
                V.tensor_reduce(out=a[0:1, 3:4], in_=stat_ps[0:1, 0:P], op=ALU.max, axis=AX_X).then_inc(wlevel, 1)
                dve.wait_ge(wlevel_mm, 2 * n + 2)
                steps.link(dve, V.tensor_copy(a[:, 0:1], stat_ps[:, 0:1]))
                steps.link(dve, V.tensor_scalar(a[:, 1:2].bitcast(I32), a[:, 0:1].bitcast(I32), 0x7F800000, None,
                                                ALU.bitwise_and))
                steps.link(dve, V.reciprocal(a[:, 2:3], a[:, 1:2]))
                V.tensor_scalar(unscale[n], a[:, 1:2], 2.0 ** -13 / X_SCALE, None, ALU.mult)
                V.tensor_scalar(wscale[n], a[:, 2:3], 2.0 ** 13, None, ALU.mult).then_inc(wlevel, 1)
                for t in range(0, TAPS, 4):
                    m = min(4, TAPS - t)
                    k = 7 * n + t // 4
                    dve.wait_ge(whigh, k + 1)
                    V.scalar_tensor_tensor(out=wconv[:, n, 1, t:t + m, :].rearrange("p t o -> p (t o)"),
                                           in0=gram_ps[k % 2][:, 0:m * P], scalar=wscale[n],
                                           in1=wconv[:, n, 0, t:t + m, :].rearrange("p t o -> p (t o)"),
                                           op0=ALU.mult, op1=ALU.subtract).then_inc(wlow, 1)

            gn1_chain, gn2_chain = Chain(gn1_link, GN_LINKS), Chain(gn2_link, GN_LINKS)
            prep_chain = Chain(prep_link, 8 * PREP_LINKS)

            def raw_chunk(slot):
                return ring[:, slot, 0:CHUNK * IMG:2]

            def raw_stats(n, c):
                s = c % 2
                dve.wait_ge(raw_in[s], 64 * (4 * n + 1 + c // 2))
                for k in range(2):
                    last = V.bn_stats(bn1[:, 2 * c + k, :], ring[:, s, k * 2 * BANK:(k + 1) * 2 * BANK:2])
                last.then_inc(bn1_done, 1)

            def gn_open(g, bn, bn_done, part, n, per):
                dve.wait_ge(bn_done, per * n + per)
                alone(dve)
                V.bn_aggr(g[:, 0:2], bn[:, :, :].rearrange("p n s -> p (n s)")).then_inc(part, 1)

            def gn_mean(g, chain, part, mm, n):
                chain.round(n)
                dve.wait_ge(mm, 2 * n + 1)
                chain.link(dve, V.tensor_copy(g[:, 2:3], stat_ps[:, 0:1]))
                chain.link(dve, V.tensor_tensor(g[:, 3:4], g[:, 0:1], g[:, 2:3], ALU.subtract))
                V.scalar_tensor_tensor(out=g[:, 3:4], in0=g[:, 3:4], scalar=g[:, 3:4], in1=g[:, 1:2],
                                       op0=ALU.mult, op1=ALU.add).then_inc(part, 1)

            def gn_close(g, chain, mm, var, root_done, done, n, scale):
                dve.wait_ge(mm, 2 * n + 2)
                V.tensor_scalar(g[:, 4:5], stat_ps[:, 1:2], EPS_GN, None, ALU.add).then_inc(var, 1)
                dve.wait_ge(root_done, n + 1)
                chain.link(dve, V.reciprocal(g[:, 6:7], g[:, 5:6]))
                chain.link(dve, V.tensor_scalar(g[:, 7:8], g[:, 4:5], g[:, 6:7], g[:, 6:7], ALU.mult, ALU.mult))
                chain.link(dve, V.tensor_scalar(g[:, 7:8], g[:, 7:8], -0.5, 1.5, ALU.mult, ALU.add))
                chain.link(dve, V.tensor_scalar(g[:, 8:9], g[:, 6:7], g[:, 7:8], scale, ALU.mult, ALU.mult))
                V.tensor_scalar(g[:, 9:10], g[:, 2:3], g[:, 8:9], -1.0, ALU.mult, ALU.mult).then_inc(done, 1)

            def split_rest(n, c):
                dve.wait_ge(high_done, 4 * n + c + 1)
                dve.wait_ge(acc_done, 4 * n + c + 1)
                raw = raw_chunk(c % 2)
                V.scalar_tensor_tensor(out=raw, in0=raw, scalar=gn1[:, 8:9],
                                       in1=xh[:, CHUNK * c:CHUNK * (c + 1), :].rearrange("p h w -> p (h w)"),
                                       op0=ALU.mult, op1=ALU.subtract).then_inc(rest_done, 1)

            def ll_lows(i, k):
                dve.wait_ge(ll_high, 3 * i + k + 1)
                if k < 2:
                    flat = [t[:, 16 * k:16 * k + 16, :].rearrange("p h w -> p (h w)") for t in (xl1, xh1)]
                    V.tensor_tensor(flat[0], conv_ps[k][:, :], flat[1], ALU.subtract).then_inc(ll_low, 1)
                else:
                    flat = [t[:, :, :].rearrange("p h w -> p (h w)") for t in (xl2, xh2)]
                    V.tensor_tensor(flat[0], conv_ps[0][:, 0:H2 * H2], flat[1], ALU.subtract).then_inc(ll_low, 1)

            def level1_out(i, k):
                if k == 0:
                    dve.wait_ge(u2_done, i + 1)
                dve.wait_ge(conv_ready, 11 * i + 2 + k)
                part = z1[:, 16 * k:16 * k + 16, :].rearrange("p h w -> p (h w)")
                V.scalar_tensor_tensor(out=part, in0=conv_ps[k][:, :], scalar=unscale[1], in1=part,
                                       op0=ALU.mult, op1=ALU.add).then_inc(z1_done, 1)

            def add_up(i, q):
                if q == 0:
                    dve.wait_ge(acc_done, 4 * i + 4)
                dve.wait_ge(up_in[q % 2], 64 * (2 * i + 1 + q // 2))
                dst = xacc[:, q // 2:H0:2, q % 2:H0:2]
                V.scalar_tensor_tensor(out=dst, in0=up[:, q % 2, :].rearrange("p (h w) -> p h w", w=H1), scalar=0.5,
                                       in1=dst, op0=ALU.mult, op1=ALU.add).then_inc(up_added, 1)

            def x1_out(i, j):
                dve.wait_ge(conv_ready, 11 * i + 4 + j)
                if j == 0:
                    dve.wait_ge(up_added, 4 * i + 4)
                    for saved in x1_saved if not first(i) else ():
                        dve.wait_ge(saved, 16 * i)
                band = (0, 1, 1, 2, 2, 3, 3, 3)[j]
                if not first(i):
                    dve.wait_ge(x2_done, 4 * i - 4 + band + 1)
                flat = [t[:, CROWS * j:CROWS * (j + 1), :].rearrange("p h w -> p (h w)") for t in (x1, xacc)]
                V.scalar_tensor_tensor(out=flat[0], in0=conv_ps[j % 2][:, :], scalar=unscale[0], in1=flat[1],
                                       op0=ALU.mult, op1=ALU.add).then_inc(x1_done, 1)
                dve.wait_ge(x1_done, 8 * i + j + 1)
                V.bn_stats(bn2[:, j, :], flat[0]).then_inc(bn2_done, 1)

            def band_units(b, r, half):
                ch = prep_chain
                sq = st_n[:, half, :]
                dve.wait_ge(n2_kept, 16 * b + 4 * r + 2 * half + 2)
                if r == 0 and half == 0:
                    ch.round(b)
                    dve.wait_ge(unit_high, START + 8 * b)
                else:
                    dve.wait_ge(unit_high, START + 8 * b + 2 * r + half)
                ch.link(dve, V.tensor_scalar(st_a[:, :], st_a[:, :], 1e-12, None, ALU.max))
                ch.link(dve, V.reciprocal(st_a[:, :], st_a[:, :]))
                ch.link(dve, V.tensor_tensor(st_b[:, :], st_a[:, :], st_a[:, :], ALU.mult))
                ch.link(dve, V.scalar_tensor_tensor(out=st_b[:, :], in0=st_b[:, :], scalar=-0.5, in1=sq,
                                                    op0=ALU.mult, op1=ALU.mult))
                ch.link(dve, V.scalar_tensor_tensor(out=st_a[:, :], in0=st_b[:, :], scalar=1.5, in1=st_a[:, :],
                                                    op0=ALU.add, op1=ALU.mult))
                ch.link(dve, V.scalar_tensor_tensor(out=sq, in0=sq, scalar=EPS_SIM ** -0.5, in1=st_a[:, :],
                                                    op0=ALU.mult, op1=ALU.mult))
                ch.link(dve, V.tensor_scalar(st_b[:, :], sq, 1.0001, None, ALU.is_lt, ALU.add,
                                             accum_out=short[:, half:half + 1]))
                part = st_x2[:, GROUPS * half:GROUPS * (half + 1), :, :].rearrange("p e h w -> p (e h w)")
                V.scalar_tensor_tensor(out=st_b[:, :], in0=part,
                                       scalar=SIM_SCALE, in1=st_a[:, :], op0=ALU.mult, op1=ALU.mult).then_inc(unit_vec, 1)

            def unit_lows(b, r, half):
                dve.wait_ge(v_high, 8 * b + 2 * r + half + 1)
                part = st_x2[:, GROUPS * half:GROUPS * (half + 1), :, :].rearrange("p e h w -> p (e h w)")
                V.scalar_tensor_tensor(out=st_v[:, 1, half, :], in0=part, scalar=X_SCALE, in1=st_v[:, 0, half, :],
                                       op0=ALU.mult, op1=ALU.subtract)
                dve.wait_ge(unit_high, START + 8 * b + 2 * r + half + 1)
                V.tensor_tensor(st_hl[:, 1, half, :], st_b[:, :], st_hl[:, 0, half, :], ALU.subtract).then_inc(unit_low, 1)

            def set_flag(b, r):
                dve.wait_ge(count_ready, 4 * b + r + 1)
                pads = PAD_EDGE if r in (0, BANDS - 1) else PAD_INNER
                V.tensor_scalar(flag[:, :], stat_ps[0:1, 0:1], float(-pads), None, ALU.add).then_inc(flag_done, 1)

            def weights(b, u, k, short_ones):
                n, e = 8 * (8 * b + u) + k, k // 2
                dve.wait_ge(gram_ready, n + 1)
                if k % 2 == 0:
                    dve.wait_ge(group_done, START + 4 * (8 * b + u) + e - 1 if (u > 0 or e > 0) else START + 32 * b)
                alone(dve)
                g = gram_ps[k % 2][0:KN, :].rearrange("p (t n) -> p t n", t=2)
                dst = wgt[:, e % 2, 2 * (k % 2):2 * (k % 2) + 2, :]
                with dve.If(short_ones > 0):
                    V.tensor_scalar(dst, guard_ps[0:KN, :].rearrange("p (t n) -> p t n", t=2), 1.0, None, ALU.min)
                    dve.drain()
                    V.tensor_tensor(g, g, dst, ALU.mult)
                    dve.drain()
                V.scalar_tensor_tensor(
                    out=dst, in0=g, scalar=SIM_SCALE ** 2,
                    in1=tapw[:, :].unsqueeze(1).to_broadcast([KN, 2, 2 * QN]), op0=ALU.add, op1=ALU.mult).then_inc(wgt_done, 1)

            def result(b, u):
                r, half = u // 2, u % 2
                dve.wait_ge(group_done, START + 4 * (8 * b + u + 1))
                if half == 0:
                    dve.wait_ge(x1_res_in, 64 * (4 * b + r + 1))
                    dve.wait_ge(stored, START + 64 * (4 * b + r))
                o = out_ps[:, :].rearrange("p (q h w) -> p q h w", q=Q, h=TH)
                for rp in range(2):
                    dst = ostage[:, rp:2 * TH:2, IMG // 2 * half:IMG // 2 * (half + 1)].rearrange("p h (w c) -> p c h w", c=2)
                    ins = V.tensor_tensor(dst, o[:, 2 * rp:2 * rp + 2], x1_res[:, 2 * rp:2 * rp + 2, :, UW * half:UW * (half + 1)],
                                          ALU.add)
                    ins.then_inc(unit_out if rp else half_out, 1)

            def iteration(i, conv, ls):
                b = i - 1
                if ls:
                    x1_out(b, CONV_TILES - 1)
                if conv:
                    split_rest(i, 3)
                if ls:
                    gn_open(gn2, bn2, bn2_done, gn2_part, b, 8)
                if conv:
                    ll_lows(i, 0)
                    ll_lows(i, 1)
                if ls:
                    gn_mean(gn2, gn2_chain, gn2_part, gn2_mm, b)
                if conv:
                    ll_lows(i, 2)
                if ls:
                    gn_close(gn2, gn2_chain, gn2_mm, gn2_var, gn2_root, gn2_done, b, 1.0)
                if conv:
                    raw_stats(i + 1, 0)
                    raw_stats(i + 1, 1)
                if ls:
                    for half in range(2):
                        band_units(b, 0, half)
                        unit_lows(b, 0, half)
                if conv:
                    level1_out(i, 0)
                    raw_stats(i + 1, 2)
                    level1_out(i, 1)
                    raw_stats(i + 1, 3)
                    gn_open(gn1, bn1, bn1_done, gn1_part, i + 1, 4)
                if ls:
                    set_flag(b, 0)
                short_ones = None
                for j in range(CONV_TILES):
                    if ls and j % 2 == 0:
                        dve.wait_ge(flag_done, START + 4 * b + j // 2 + 1)
                        alone(dve)
                        short_ones = dve.value_load(flag[0:1, 0:1], min_val=0, max_val=2 * P * UN)
                    for k in range(PAIRS):
                        if ls:
                            weights(b, j, k, short_ones)
                        if k == 0:
                            if conv and j > 0:
                                x1_out(i, j - 1)
                            if ls and j > 0:
                                result(b, j - 1)
                        if ls and k in (2, 4) and j in (0, 2, 4):
                            r = 1 + j // 2
                            band_units(b, r, k // 2 - 1)
                        if ls and k in (3, 5) and j in (0, 2, 4):
                            unit_lows(b, 1 + j // 2, k // 2 - 1)
                        if ls and k == 7 and j in (1, 3, 5):
                            set_flag(b, 1 + j // 2)
                        if conv and k in (3, 4, 5, 6) and j == 0:
                            add_up(i, k - 3)
                        if conv and k == 7 and j == 0:
                            gn_mean(gn1, gn1_chain, gn1_part, gn1_mm, i + 1)
                        if conv and k == 3 and j == 1:
                            gn_close(gn1, gn1_chain, gn1_mm, gn1_var, gn1_root, gn1_done, i + 1, X_SCALE)
                        if conv and k == 3 and j in (3, 5, 7):
                            split_rest(i + 1, j // 2 - 1)
                if ls:
                    result(b, CONV_TILES - 1)

            for c in range(CHUNKS):
                raw_stats(0, c)
            gn_open(gn1, bn1, bn1_done, gn1_part, 0, 4)
            gn_mean(gn1, gn1_chain, gn1_part, gn1_mm, 0)
            gn_close(gn1, gn1_chain, gn1_mm, gn1_var, gn1_root, gn1_done, 0, X_SCALE)
            for c in range(CHUNKS - 1):
                split_rest(0, c)
            iteration(0, True, False)
            with dve.Fori(1, B) as i:
                iteration(i, True, True)
            iteration(B, False, True)

        @block.tensor
        def _(pe):
            mm = nc.tensor.matmul
            pe.sem_inc(group_done, START)
            pe.wait_ge(const_in, 16 * 9)
            pe.wait_ge(zeroed, 2)
            for n in range(3):
                w = wraw[n].rearrange("o (i t) -> o t i", t=TAPS)
                pe.wait_ge(wraw_in[n], 16)
                for t in range(0, TAPS, 4):
                    k = 7 * n + t // 4
                    if k >= 2:
                        pe.wait_ge(wmix_kept, k - 1)
                    for s in range(t, min(t + 4, TAPS)):
                        last = mm(conv_ps[k % 2][:, (s - t) * P:(s - t + 1) * P], w[:, s, :], mix, start=True, stop=True)
                    last.then_inc(wmixed, 1)
                pe.wait_ge(wlevel, 3 * n + 1)
                nc.tensor.transpose(stat_ps[0:1, 0:P], gn1[:, 2:3], ident).then_inc(wlevel_mm, 1)
                pe.wait_ge(wlevel, 3 * n + 2)
                for g in range(4):
                    last = mm(stat_ps[C * g:C * g + C, 0:1], ones_row, gn1[0:1, 3:4], start=True, stop=True)
                last.then_inc(wlevel_mm, 1)
                pe.wait_ge(wmix_kept, 7 * n + 7)
                for t in range(0, TAPS, 4):
                    k = 7 * n + t // 4
                    m = min(4, TAPS - t)
                    if k >= 2:
                        pe.wait_ge(wlow, k - 1)
                    mm(gram_ps[k % 2][:, 0:m * P], mix, wmix[:, t * P:(t + m) * P], start=True, stop=True).then_inc(wfull, 1)

            def low_pass(dst, high, low, r0, r1, side):
                first = True
                for q in range(Q):
                    for t in (high, low):
                        src = t[:, 2 * r0 + q // 2:2 * r1:2, q % 2:2 * side:2]
                        last = mm(dst, gat_c[:, q, :], src, start=first, stop=(q == Q - 1 and t is low))
                        first = False
                return last

            def conv(level, dst, high, low, r0, nr, side, hook=None):
                taps = sorted(range(TAPS), key=lambda t: t != TAPS // 2)
                n = 0
                for t in taps:
                    dy, dx = t // K - K // 2, t % K - K // 2
                    a0, a1 = max(r0, -dy), min(r0 + nr, side - dy)
                    b0, b1 = max(0, -dx), min(side, side - dx)
                    for w, src in ((0, high), (0, low), (1, high)):
                        if hook:
                            hook(n)
                        last = mm(dst[:, a0 - r0:a1 - r0, b0:b1], wconv[:, level, w, t, :],
                                  src[:, a0 + dy:a1 + dy, b0 + dx:b1 + dx], start=(n == 0), stop=(n == 3 * TAPS - 1))
                        n += 1
                last.then_inc(conv_ready, 1)

            def gn_products(g, part, done, n, k):
                pe.wait_ge(part, 2 * n + k + 1)
                mm(stat_ps[:, k:k + 1], average, g[:, 0:1] if k == 0 else g[:, 3:4], start=True, stop=True).then_inc(done, 1)

            def norm_piece(b, r, p):
                half, k = p // 2, p % 2
                pe.wait_ge(sq_done, 8 * b + 2 * r + half + 1)
                if p > 0:
                    pe.wait_ge(n2_kept, 16 * b + 4 * r + p)
                mm(stat_ps[:, 0:PIECE], same_quadrant, st_n[:, half, k * PIECE:(k + 1) * PIECE], start=True, stop=True)\
                    .then_inc(n2_ready, 1)

            def count_short(b, r, gn1_rounds=None):
                if gn1_rounds is not None:
                    pe.wait_ge(gn1_var, gn1_rounds)
                pe.wait_ge(unit_vec, START + 8 * b + 2 * r + 2)
                for half in range(2):
                    last = mm(stat_ps[0:1, 0:1], short[:, half:half + 1], ones[:, :], start=(half == 0), stop=(half == 1))
                last.then_inc(count_ready, 1)

            def key_values(b, u, part):
                s = u % 2
                pe.wait_ge(unit_in[s], 192 * (4 * b + u // 2 + 1))
                pe.wait_ge(vals_done, START + 16 * b + 2 * u + part)
                alone(pe)
                for e in (2 * part, 2 * part + 1):
                    for g in range(BANDS):
                        for q in range(Q):
                            n, row = ((e % 2) * BANDS + g) * 2 + q // 2, 64 * (q % 2)
                            last = mm(vals_ps[row:row + KQ, C * n:C * n + C],
                                      values[s][0:2 * C, q, e, TH * KW * g:TH * KW * g + KQ], unpair_c[:, :],
                                      start=True, stop=True)
                last.then_inc(vt_ready, 1)

            def gram(b, u, k, short_ones):
                s, e, n = u % 2, k // 2, 8 * (8 * b + u) + k
                pe.wait_ge(wgt_done, START + n - 1 if (u > 0 or k > 1) else START + 64 * b)

                def products(bank, key, query, e_at):
                    for t in range(2):
                        g = 2 * (k % 2) + t
                        window = query[:, :, e_at, :].rearrange("p q (h w) -> p q h w", w=KW)
                        for q in range(Q):
                            row, col = 64 * (q % 2), (2 * t + q // 2) * QN
                            last = mm(bank[row:row + KQ, col:col + QN], key[:, q, e_at, TH * KW * g:TH * KW * g + KQ],
                                      window[:, :, TH * g + 1:TH * g + 1 + TH, 1:1 + TW], start=True, stop=True)
                    return last

                with pe.If(short_ones > 0):
                    pe.wait_ge(wgt_done, START + n)
                    row = 64 + C * (e // 2)
                    norm = norm_rows[s][row:row + 1]
                    products(guard_ps, norm, norm, e % 2)
                last = products(gram_ps[k % 2], keys[s], queries[s], e)
                last.then_inc(gram_ready, 1)

            def filter_group(b, u, e):
                if e == 0:
                    pe.wait_ge(unit_out, START + 8 * b + u)
                pe.wait_ge(vals_done, START + 16 * b + 2 * u + e // 2 + 1)
                pe.wait_ge(wgt_done, START + 8 * (8 * b + u) + 2 * e + 2)
                o = out_ps[:, :].rearrange("p (q h w) -> p q h w", q=Q, h=TH)
                for c in range(2):
                    for g in range(BANDS):
                        last = mm(o[C * g:C * g + C, :, :, TW * e:TW * e + TW], vals[:, (e * BANDS + g) * 2 + c, :],
                                  wgt[:, e % 2, g, c * QN:(c + 1) * QN], start=(c == 0), stop=(c == 1))
                last.then_inc(group_done, 1)

            def iteration(i, conv_on, ls):
                b = i - 1
                short_ones = [None]
                if conv_on:
                    pe.wait_ge(low_done, 4 * i + 2)
                    if not first(i):
                        pe.wait_ge(x1_done, 8 * i - 1)
                    ll = [conv_ps[k][:, :].rearrange("p (h w) -> p h w", w=H1) for k in range(2)]
                    low_pass(ll[0], xh, xl, 0, 16, H1).then_inc(ll_ready, 1)
                    pe.wait_ge(low_done, 4 * i + 4)
                    if not first(i):
                        pe.wait_ge(x1_done, 8 * i)
                    low_pass(ll[1], xh, xl, 16, 32, H1).then_inc(ll_ready, 1)
                if ls:
                    pe.wait_ge(gn1_var, i + 1) if conv_on else None
                    pe.wait_ge(flag_done, START + 4 * b)
                    gn_products(gn2, gn2_part, gn2_mm, b, 0)
                if conv_on:
                    pe.wait_ge(ll_low, 3 * i + 2)
                    t2 = conv_ps[0][:, 0:H2 * H2].rearrange("p (h w) -> p h w", w=H2)
                    low_pass(t2, xh1, xl1, 0, H2, H2).then_inc(ll_ready, 1)
                if ls:
                    gn_products(gn2, gn2_part, gn2_mm, b, 1)
                if conv_on:
                    pe.wait_ge(ll_low, 3 * i + 3)
                    conv(2, conv_ps[1][:, 0:H2 * H2].rearrange("p (h w) -> p h w", w=H2), xh2, xl2, 0, H2, H2)

                def hook_1a(n):
                    if ls and n in (8, 16, 24, 32):
                        if n == 8:
                            pe.wait_ge(gn2_var, b + 1)
                        norm_piece(b, 0, n // 8 - 1)

                def hook_1b(n):
                    if ls and n == 56:
                        count_short(b, 0)

                if conv_on:
                    conv(1, ll[0], xh1, xl1, 0, 16, H1, hook_1a)
                    pe.wait_ge(z2_done, i + 1)
                    conv(1, ll[1], xh1, xl1, 16, 16, H1, hook_1b)
                else:
                    for n in range(3 * TAPS):
                        hook_1a(n)
                    for n in range(3 * TAPS):
                        hook_1b(n)

                for j in range(CONV_TILES):
                    def hook(n, j=j):
                        if n not in HOOKS:
                            return
                        k = n // 8
                        if ls:
                            if k == 0:
                                if j % 2 == 0:
                                    pe.wait_ge(flag_done, START + 4 * b + j // 2 + 1)
                                    alone(pe)
                                    short_ones[0] = pe.value_load(flag[0:1, 0:1], min_val=0, max_val=2 * P * UN)
                                key_values(b, j, 0)
                            if k == 4:
                                key_values(b, j, 1)
                            if k < PAIRS:
                                gram(b, j, k, short_ones[0])
                            if k in (3, 5, 7, 8):
                                filter_group(b, j, (k - 3) // 2 if k < 8 else 3)
                            if j in (0, 2, 4) and k in (1, 2, 3, 4):
                                if k == 1:
                                    pe.wait_ge(flag_done, START + 4 * b + j // 2 + 1)
                                norm_piece(b, 1 + j // 2, k - 1)
                            if j in (1, 3, 5) and k == 6:
                                count_short(b, 1 + j // 2, i + 2 if conv_on and j == 1 else None)
                        if conv_on:
                            if j == 0 and k in (5, 8):
                                if k == 5 and ls:
                                    pe.wait_ge(n2_kept, 16 * b + 8)
                                gn_products(gn1, gn1_part, gn1_mm, i + 1, k // 8)

                    if conv_on:
                        if j < 2:
                            pe.wait_ge(z1_done, 2 * i + 1 + j)
                        else:
                            pe.wait_ge(x1_done, 8 * i + j - 1)
                        conv(0, conv_ps[j % 2][:, :].rearrange("p (h w) -> p h w", w=H0), xh, xl, CROWS * j, CROWS, H0, hook)
                    else:
                        for n in range(3 * TAPS):
                            hook(n)

            gn_products(gn1, gn1_part, gn1_mm, 0, 0)
            gn_products(gn1, gn1_part, gn1_mm, 0, 1)
            iteration(0, True, False)
            with pe.Fori(1, B) as i:
                iteration(i, True, True)
            iteration(B, False, True)


def const_arrays():
    return dict(zip(("square", "gather", "taps", "unpair"), host_constants()))


_INS = ["x", "L0_conv_w0", "L0_conv_w1", "L0_conv_w2", "L0_conv_bias", "L1_conv_spatial_weight"]


def kernel(**inputs):
    import concourse.bacc as bacc
    from concourse.bass_utils import run_bass_kernel_spmd as run

    nc = bacc.Bacc("TRN2", target_bir_lowering=False, num_devices=1)
    arrays = {n: np.ascontiguousarray(inputs[n]) for n in _INS} | const_arrays()
    args = [nc.dram_tensor(f"in_{n}", a.shape, mybir.dt.from_np(a.dtype), kind="ExternalInput").ap() for n, a in arrays.items()]
    args.append(nc.dram_tensor("out_0", inputs["x"].shape, F32, kind="ExternalOutput").ap())
    build(nc, *args)
    r = run(nc, [{f"in_{n}": a for n, a in arrays.items()}], core_ids=[0])
    return r.results[0]["out_0"]
```

```python
from contextlib import ExitStack

import numpy as np

import concourse.bass as bass
from concourse import mybir

F32 = mybir.dt.float32
F16 = mybir.dt.float16
I32 = mybir.dt.int32
ALU = mybir.AluOpType
ACT = mybir.ActivationFunctionType
AX_X = mybir.AxisListType.X

P = 128
C = 32
Q = 4
B = 8
IMG = 128
H0, H1, H2 = IMG // 2, IMG // 4, IMG // 8
K = 5
TAPS = K * K
BANK = 512
CONV_TILES = H0 * H0 // BANK
CROWS = H0 // CONV_TILES
CHUNK = 16
CHUNKS = H0 // CHUNK
PARTS = [(0, 16), (16, 32), (32, 48), (48, 54), (54, 64)]
NP = len(PARTS)
W_SCALE = 2.0 ** 12
X_SCALE = 32.0
SIM_SCALE = 64.0
EPS_GN = 1e-5
EPS_SIM = 1e-8

TH, TW = 4, 8
QN = Q * TH * TW
KH, KW = TH + 2, TW + 2
KQ = KH * KW
KN = 64 + KQ
BANDS = 4
BH, UW = H0 // BANDS, H0 // 2
SH = BH + 2
STRIPS = H0 // TW
SN = SH * KW
GROUPS = UW // TW
UN = GROUPS * SN
PIECE = UN // 2
PAIRS = 2 * GROUPS
START = 1
HOOKS = [9 * n for n in range(8)] + [3 * TAPS]

PAD_EDGE = P * (SH + GROUPS * KW - 1)
PAD_INNER = P * SH

NORMS_AT = [8, 20, 32, 66]
COUNTS_AT = [100, 140]
GN_LINKS = 5
PREP_LINKS = 5


def host_constants():
    haar = np.array([[1, 1, 1, 1], [1, 1, -1, -1], [1, -1, 1, -1], [1, -1, -1, 1]], np.float32)
    mix = np.zeros((P, P), np.float32)
    gather = np.zeros((P, Q, P), np.float16)
    for c in range(C):
        for t in range(Q):
            for q in range(Q):
                mix[4 * c + t, C * q + c] = 0.5 * haar[t, q]
                gather[C * q + c, t, C * t + c] = 0.5
    part = np.arange(P)
    average = np.where(part[:, None] % C == part[None] % C, 0.25, 0).astype(np.float32)
    same_quadrant = (part[:, None] // C == part[None] // C).astype(np.float32)
    square = np.stack([mix, average, same_quadrant, np.eye(P, dtype=np.float32)], 1)
    unpair = np.zeros((2 * C, C), np.float16)
    unpair[np.arange(2 * C), np.arange(2 * C) % C] = 1 / X_SCALE
    q, h, w = np.meshgrid(np.arange(Q), np.arange(TH), np.arange(TW), indexing="ij")
    qr, qc = (2 * h + q // 2).ravel(), (2 * w + q % 2).ravel()
    taps = np.zeros((KN, TAPS, 2, QN), np.float16)
    h, w = np.meshgrid(np.arange(KH), np.arange(KW), indexing="ij")
    for k in range(Q):
        dr = (2 * (h - 1) + k // 2).reshape(-1, 1) - qr[None]
        dc = (2 * (w - 1) + k % 2).reshape(-1, 1) - qc[None]
        for t in range(TAPS):
            taps[64 * (k % 2):64 * (k % 2) + KQ, t, k // 2] = (dr == t // K - K // 2) & (dc == t % K - K // 2)
    return square, gather, taps.reshape(KN, TAPS * 2 * QN), unpair


def first(n):
    return isinstance(n, int) and n == 0


class Chain:

    def __init__(self, sem, per_round):
        self.sem, self.per_round, self.base, self.k = sem, per_round, 0, 0

    def round(self, n):
        self.base, self.k = n * self.per_round, 0

    def link(self, engine, instruction):
        self.k += 1
        assert self.k <= self.per_round
        instruction.then_inc(self.sem, 1)
        engine.wait_ge(self.sem, self.base + self.k)


def build(nc, x, w0, w1, w2, bias, spatial, square, gather, tapmask, unpair, out):
    ctx = ExitStack()
    with ctx:
        def sb(name, shape, dt):
            return ctx.enter_context(nc.sbuf_tensor(name, shape, dt))

        def psum(name):
            return ctx.enter_context(nc.psum_tensor(name, [P, BANK], F32))

        def sem(name):
            return ctx.enter_context(nc.semaphore(name))

        wconv = sb("wconv", [P, 3, 2, TAPS, P], F16)
        xh, xl = sb("xh", [P, H0, H0], F16), sb("xl", [P, H0, H0], F16)
        xh1, xl1 = sb("xh1", [P, H1, H1], F16), sb("xl1", [P, H1, H1], F16)
        xh2, xl2 = sb("xh2", [P, H2, H2], F16), sb("xl2", [P, H2, H2], F16)
        ring = sb("ring", [P, 2, CHUNK * IMG], F32)
        xacc = sb("xacc", [P, H0, H0], F32)
        x1 = sb("x1", [P, H0, H0], F32)
        unit_mem = sb("unit_mem", [P, 2, 3 * Q * UN], F16)
        x1_res = sb("x1_res", [P, Q, TH, H0], F32)
        st_x2 = sb("st_x2", [P, STRIPS, SH, KW], F32)
        st_v = sb("st_v", [P, 2, 2, UN], F16)
        st_hl = sb("st_hl", [P, 2, 2, UN], F16)
        st_n = sb("st_n", [P, 2, UN], F32)
        st_a, st_b = sb("st_a", [P, UN], F32), sb("st_b", [P, UN], F32)
        wgt = sb("wgt", [KN, 2, BANDS, 2 * QN], F32)
        vals = sb("vals", [KN, 2 * BANDS * GROUPS, C], F32)
        ostage = sb("ostage", [P, 2 * TH, IMG], F32)
        z2 = sb("z2", [P, H2 * H2], F32)
        z1 = sb("z1", [P, H1, H1], F32)
        up = sb("up", [P, 2, H1 * H1], F32)
        tapw = sb("tapw", [KN, 2 * QN], F32)
        sq_c = sb("sq_c", [P, 4, P], F32)
        gat_c = sb("gat_c", [P, Q, P], F16)
        unpair_c = sb("unpair_c", [2 * C, C], F16)
        bn1, bn2 = sb("bn1", [P, CONV_TILES, 6], F32), sb("bn2", [P, CONV_TILES, 6], F32)
        gn1, gn2 = sb("gn1", [P, 10], F32), sb("gn2", [P, 10], F32)
        small = sb("small", [P, 7], F32)
        spat = sb("spat", [P, TAPS], F32)
        short = sb("short", [P, 2], F32)
        flag = sb("flag", [1, 2], I32)
        tiny = sb("tiny", [P, 1], F32)
        ones = sb("ones", [P, 1], F32)
        mix, average, same_quadrant, ident = (sq_c[:, n, :] for n in range(4))
        unscale = [small[:, n:n + 1] for n in range(3)]
        wscale = [small[:, 3 + n:4 + n] for n in range(3)]
        biasq = small[:, 6:7]
        ones_row = sq_c[0:1, 2, 0:C]

        def unit_part(s, n):
            return unit_mem[:, s, n * Q * UN:(n + 1) * Q * UN].rearrange("p (q e n) -> p q e n", q=Q, e=GROUPS)

        keys, queries, values = ([unit_part(s, n) for s in range(2)] for n in range(3))
        norm_rows = [unit_mem[:, s, 2 * Q * UN:3 * Q * UN].bitcast(F32).rearrange("p (q e n) -> p q e n", q=Q, e=2)
                     for s in range(2)]
        wraw = [unit_mem[:, 0, 0:2 * TAPS * P].bitcast(F32), unit_mem[:, 1, 0:2 * TAPS * P].bitcast(F32), x1[:, :, :].rearrange("p a b -> p (a b)")[:, 0:TAPS * P]]
        wmix = xacc[:, :, :].rearrange("p a b -> p (a b)")[:, 0:TAPS * P]
        tap_c = unit_mem[0:KN, 0, 0:TAPS * 2 * QN]

        conv_ps = [psum("conv0"), psum("conv1")]
        gram_ps = [psum("gram0"), psum("gram1")]
        vals_ps, out_ps, guard_ps, stat_ps = psum("vals_ps"), psum("out_ps"), psum("guard_ps"), psum("stat_ps")

        def dram(name, shape, dt):
            return nc.dram_tensor(name, shape, dt, kind="Internal").ap()

        d_z2, d_z1 = dram("d_z2", [B, P, H2 * H2], F32), dram("d_z1", [B, P, H1 * H1], F32)
        d_x1 = dram("d_x1", [B, P, H0 * H0], F32)
        d_hl = dram("d_hl", [B, 2 * BANDS, P, 2, UN], F16)
        d_v = dram("d_v", [B, 2 * BANDS, P, 2, UN], F16)
        d_n = dram("d_n", [B, 2 * BANDS, Q, UN], F32)

        passed = sem("passed")
        square_in = sem("square_in")
        const_in = sem("const_in")
        wraw_in = [sem(f"wraw_in{n}") for n in range(3)]
        wmixed = sem("wmixed")
        wmix_kept = sem("wmix_kept")
        wlevel = sem("wlevel")
        wlevel_mm = sem("wlevel_mm")
        wfull = sem("wfull")
        whigh = sem("whigh")
        wlow = sem("wlow")
        setup = sem("setup")
        zeroed = sem("zeroed")
        taps_in = sem("taps_in")
        tapw_done = sem("tapw_done")
        raw_in = [sem("raw_in0"), sem("raw_in1")]
        bn1_done = sem("bn1_done")
        gn1_part, gn2_part = sem("gn1_part"), sem("gn2_part")
        gn1_mm, gn2_mm = sem("gn1_mm"), sem("gn2_mm")
        gn1_var, gn2_var = sem("gn1_var"), sem("gn2_var")
        gn1_root, gn2_root = sem("gn1_root"), sem("gn2_root")
        gn1_link, gn2_link = sem("gn1_link"), sem("gn2_link")
        gn1_done, gn2_done = sem("gn1_done"), sem("gn2_done")
        high_done = sem("high_done")
        acc_done = sem("acc_done")
        rest_done = sem("rest_done")
        low_done = sem("low_done")
        ll_ready = sem("ll_ready")
        ll_high = sem("ll_high")
        ll_low = sem("ll_low")
        conv_ready = sem("conv_ready")
        z2_done = sem("z2_done")
        z2_saved, z1_saved = sem("z2_saved"), sem("z1_saved")
        up2_in = sem("up2_in")
        u2_done = sem("u2_done")
        z1_done = sem("z1_done")
        up_in = [sem("up_in0"), sem("up_in1")]
        up_added = sem("up_added")
        x1_done = sem("x1_done")
        x1_saved = [sem(f"x1_saved{r}") for r in range(BANDS)]
        bn2_done = sem("bn2_done")
        pad_zero = sem("pad_zero")
        x2_done = sem("x2_done")
        sq_done = sem("sq_done")
        v_high = sem("v_high")
        n2_ready = sem("n2_ready")
        n2_kept = sem("n2_kept")
        prep_link = sem("prep_link")
        unit_vec = sem("unit_vec")
        unit_high = sem("unit_high")
        value_low = sem("value_low")
        unit_low = sem("unit_low")
        count_ready = sem("count_ready")
        flag_done = sem("flag_done")
        half_saved = sem("half_saved")
        unit_in = [sem("unit_in0"), sem("unit_in1")]
        x1_res_in = sem("x1_res_in")
        vt_ready = sem("vt_ready")
        vals_done = sem("vals_done")
        gram_ready = sem("gram_ready")
        wgt_done = sem("wgt_done")
        group_done = sem("group_done")
        unit_out = sem("unit_out")
        stored = sem("stored")

        def raw_part(k):
            r0, r1 = PARTS[k]
            return ring[:, r0 // CHUNK % 2, r0 % CHUNK * IMG:(r0 % CHUNK + r1 - r0) * IMG:2]

        def alone(engine):
            engine.sem_inc(passed, 1)

        block = ctx.enter_context(nc.Block())

        @block.sync
        def _(sp):
            sp.sem_inc(half_saved, START)
            sp.sem_inc(stored, START)
            sp.dma_start(sq_c[:, :, :], square).then_inc(square_in, 16)
            for n, w in enumerate((w0, w1, w2)):
                sp.dma_start(wraw[n], w.rearrange("o i a b -> o (i a b)")).then_inc(wraw_in[n], 16)
            sp.dma_start(gat_c[:, :, :], gather).then_inc(const_in, 16)
            for q in range(Q):
                sp.dma_start(small[C * q:C * q + C, 6:7], bias.rearrange("(c a) -> c a", a=1)).then_inc(const_in, 16)
            sp.dma_start(spat[:, :], spatial.rearrange("(a k) -> a k", a=1).to_broadcast([P, TAPS])).then_inc(const_in, 16)
            sp.dma_start(unpair_c[:, :], unpair).then_inc(const_in, 16)
            sp.wait_ge(wmixed, 7)
            sp.wait_ge(wlevel, 1)
            sp.dma_start(tap_c, tapmask).then_inc(taps_in, 16)

            def save_half(b, h):
                sp.wait_ge(unit_low, START + 8 * b + h + 1)
                sp.dma_start(d_hl[b, h], st_hl[:, :, h % 2, :]).then_inc(half_saved, 16)
                sp.dma_start(d_v[b, h], st_v[:, :, h % 2, :]).then_inc(half_saved, 16)
                sp.dma_start(d_n[b, h], st_n[0:P:C, h % 2, :]).then_inc(half_saved, 16)

            def load_unit(b, u):
                s = u % 2
                sp.wait_ge(half_saved, START + 48 * (8 * b + u + 1))
                alone(sp)
                if u >= 2:
                    sp.wait_ge(group_done, START + 4 * (8 * b + u - 1))
                else:
                    sp.wait_ge(group_done, START + 32 * b)
                for dst, order in ((keys[s], (0, 1, 0, 1)), (queries[s], (0, 0, 1, 1))):
                    for j, hl in enumerate(order):
                        sp.dma_start(dst[C * j:C * j + C].rearrange("c q e n -> c q (e n)"),
                                     d_hl[b, u, :, hl, :].rearrange("(q c) n -> c q n", c=C)).then_inc(unit_in[s], 16)
                for hl in range(2):
                    sp.dma_start(values[s][C * hl:C * hl + C].rearrange("c q e n -> c q (e n)"),
                                 d_v[b, u, :, hl, :].rearrange("(q c) n -> c q n", c=C)).then_inc(unit_in[s], 16)
                for g in range(2):
                    sp.dma_start(norm_rows[s][64 + C * g:65 + C * g].rearrange("a q e n -> a q (e n)"),
                                 d_n[b, u, :, UN // 2 * g:UN // 2 * (g + 1)].rearrange("(a q) n -> a q n", a=1))\
                        .then_inc(unit_in[s], 16)

            def load_residual(b, r):
                sp.wait_ge(x1_saved[r], 16 * b + 16)
                alone(sp)
                sp.wait_ge(unit_out, START + 8 * b + 2 * r)
                src = d_x1[b].rearrange("(q c) (h w) -> c q h w", c=C, w=H0)
                for g in range(BANDS):
                    row = BH * r + TH * g
                    sp.dma_start(x1_res[C * g:C * g + C].rearrange("c q h w -> c q (h w)"),
                                 src[:, :, row:row + TH, :].rearrange("c q h w -> c q (h w)")).then_inc(x1_res_in, 16)

            def store_band(b, r):
                sp.wait_ge(unit_out, START + 8 * b + 2 * r + 2)
                for g in range(BANDS):
                    row = 2 * (BH * r + TH * g)
                    sp.dma_start(out[b, :, row:row + 2 * TH, :].rearrange("c h w -> c (h w)"),
                                 ostage[C * g:C * g + C].rearrange("c h w -> c (h w)")).then_inc(stored, 16)

            def iteration(b):
                save_half(b, 0)
                load_unit(b, 0)
                load_residual(b, 0)
                save_half(b, 1)
                load_unit(b, 1)
                for u in range(2 * BANDS):
                    if u % 2 == 0 and u > 0:
                        store_band(b, u // 2 - 1)
                        load_residual(b, u // 2)
                    if u + 2 < 2 * BANDS:
                        save_half(b, u + 2)
                        load_unit(b, u + 2)
                store_band(b, BANDS - 1)

            sp.wait_ge(tapw_done, 1)
            with sp.Fori(1, B + 1) as i:
                iteration(i - 1)
            sp.wait_ge(stored, START + 4 * 64 * B)

        @block.gpsimd
        def _(pool):
            nc.gpsimd.memset(ones[:, :], 1.0).then_inc(zeroed, 1)
            nc.gpsimd.memset(tiny[:, :], 1e-24).then_inc(zeroed, 1)
            nc.gpsimd.memset(st_x2[:, :, :, :], 0.0).then_inc(zeroed, 1)

            def load_raw(batch, c, slot):
                alone(pool)
                for q in range(Q):
                    cp = q % 2
                    src = x[batch].rearrange("c (h a) w -> c a h w", a=2)[:, q // 2, CHUNK * c:CHUNK * (c + 1), cp:IMG]
                    dst = ring[C * q:C * q + C, slot, :].rearrange("p (h w) -> p h w", w=IMG)[:, :, 0:IMG - cp]
                    pool.dma_start(dst, src).then_inc(raw_in[slot], 16)

            def raw_for_stats(n, batch, cs):
                for c in cs:
                    if c >= 2:
                        pool.wait_ge(bn1_done, 4 * n + c - 1)
                    elif not first(n):
                        pool.wait_ge(low_done, NP * (n - 1) + (3, NP)[c])
                    load_raw(batch, c, c % 2)

            def raw_for_split(n, batch, cs):
                for c in cs:
                    if c < 2:
                        pool.wait_ge(bn1_done, 4 * n + 3 + c)
                    else:
                        pool.wait_ge(low_done, NP * n + c - 1)
                    load_raw(batch, c, c % 2)

            def iteration(i, nxt, conv, ls):
                b = i - 1
                if ls:
                    pool.wait_ge(x1_done, 8 * b + 8)
                    pool.dma_start(d_x1[b, :, 3 * BH * H0:], x1[:, 3 * BH:, :].rearrange("p h w -> p (h w)")).then_inc(x1_saved[3], 16)
                if conv:
                    raw_for_stats(i + 1, nxt, (0, 1))
                    pool.wait_ge(z2_done, i + 1)
                    pool.dma_start(d_z2[i], z2[:, :]).then_inc(z2_saved, 16)
                    pool.wait_ge(z2_saved, 16 * i + 16)
                    if not first(i):
                        pool.wait_ge(up_added, 4 * i)
                    alone(pool)
                    for q in range(Q):
                        pool.dma_start(up[C * q:C * q + C, 0, :].rearrange("c (q n) -> c q n", q=Q),
                                       d_z2[i].rearrange("(q c) n -> c q n", c=C)).then_inc(up2_in, 16)
                    raw_for_stats(i + 1, nxt, (2, 3))
                    pool.wait_ge(z1_done, 2 * i + 2)
                    pool.dma_start(d_z1[i], z1[:, :, :].rearrange("p h w -> p (h w)")).then_inc(z1_saved, 16)
                    pool.wait_ge(z1_saved, 16 * i + 16)
                    for q1 in range(Q):
                        if q1 >= 2:
                            pool.wait_ge(up_added, 4 * i + q1 - 1)
                        elif q1 == 0:
                            pool.wait_ge(u2_done, i + 1)
                        alone(pool)
                        for q in range(Q):
                            pool.dma_start(up[C * q:C * q + C, q1 % 2, :], d_z1[i, C * q1:C * q1 + C, :])\
                                .then_inc(up_in[q1 % 2], 16)
                    raw_for_split(i + 1, nxt, (0, 1))
                    for r in range(BANDS - 1):
                        pool.wait_ge(x1_done, 8 * i + 2 * r + 2)
                        pool.dma_start(d_x1[i, :, r * BH * H0:(r + 1) * BH * H0],
                                       x1[:, r * BH:(r + 1) * BH, :].rearrange("p h w -> p (h w)")).then_inc(x1_saved[r], 16)
                        if r == 1:
                            raw_for_split(i + 1, nxt, (2,))
                    raw_for_split(i + 1, nxt, (3,))

            raw_for_stats(0, 0, range(CHUNKS))
            raw_for_split(0, 0, range(CHUNKS))
            iteration(0, 1, True, False)
            with pool.Fori(1, B - 1) as i:
                iteration(i, i + 1, True, True)
            iteration(B - 1, 0, True, True)
            iteration(B, 0, False, True)
            pool.wait_ge(z2_saved, 16 * B)
            pool.wait_ge(z1_saved, 16 * B)
            for saved in x1_saved:
                pool.wait_ge(saved, 16 * B)
            pool.wait_ge(half_saved, START + 8 * 48 * B)

        @block.scalar
        def _(act):
            def copy(dst, src, scale=1.0, bias=0.0, func=ACT.Identity):
                return nc.scalar.activation(dst, src, func, bias=bias, scale=scale)

            act.sem_inc(n2_kept, START)
            act.sem_inc(vals_done, START)
            act.wait_ge(zeroed, 3)
            def rows(t, k):
                return t[:, PARTS[k][0]:PARTS[k][1], :].rearrange("p h w -> p (h w)")

            def split_high(n, k):
                c = PARTS[k][0] // CHUNK
                act.wait_ge(gn1_done, n + 1)
                act.wait_ge(raw_in[c % 2], 64 * (4 * n + 3 + c // 2))
                if not first(n):
                    act.wait_ge(conv_ready, 11 * (n - 1) + 3 + min((PARTS[k][1] + 1) // CROWS + 1, CONV_TILES))
                    act.wait_ge(x1_done, 8 * (n - 1) + -(-PARTS[k][1] // CROWS))
                copy(rows(xh, k), raw_part(k), scale=gn1[:, 8:9], bias=gn1[:, 9:10]).then_inc(high_done, 1)
                copy(rows(xacc, k), raw_part(k), bias=biasq).then_inc(acc_done, 1)

            def split_low(n, k):
                act.wait_ge(rest_done, NP * n + k + 1)
                copy(rows(xl, k), raw_part(k), bias=gn1[:, 9:10]).then_inc(low_done, 1)

            def root(g, var, done, n):
                act.wait_ge(var, n + 1)
                copy(g[:, 5:6], g[:, 4:5], func=ACT.Abs_reciprocal_sqrt).then_inc(done, 1)

            def ll_highs(i, k):
                act.wait_ge(ll_ready, 3 * i + k + 1)
                if k < 2:
                    copy(xh1[:, 16 * k:16 * k + 16, :].rearrange("p h w -> p (h w)"), conv_ps[k][:, :]).then_inc(ll_high, 1)
                else:
                    copy(xh2[:, :, :].rearrange("p h w -> p (h w)"), conv_ps[0][:, 0:H2 * H2]).then_inc(ll_high, 1)

            def half_in(b, h):
                r, half = h // 2, h % 2
                act.wait_ge(gn2_done, b + 1)
                if r == 0:
                    act.wait_ge(pad_zero, START + 4 * b)
                elif r == BANDS - 1:
                    act.wait_ge(pad_zero, START + 4 * b + 1 + half)
                act.wait_ge(half_saved, START + 48 * (8 * b + h - 1 if h >= 2 else 8 * b))
                lo, hi = max(BH * r - 1, 0), min(BH * r + BH + 1, H0)
                d = lo - (BH * r - 1)
                for e0, e1 in ((0, 1), (1, GROUPS)) if half == 0 else ((GROUPS, STRIPS - 1), (STRIPS - 1, STRIPS)):
                    c0, c1 = max(TW * e0 - 1, 0), min(TW * e0 + TW + 1, H0)
                    dc = c0 - (TW * e0 - 1)
                    src = x1[:, lo:hi, c0:c1]
                    src = bass.AP(src.tensor, src.offset, [src.ap[0], [TW, e1 - e0], src.ap[1], src.ap[2]])
                    last = copy(st_x2[:, e0:e1, d:d + hi - lo, dc:dc + c1 - c0], src, scale=gn2[:, 8:9], bias=gn2[:, 9:10])
                last.then_inc(x2_done, 1)
                act.wait_ge(x2_done, 8 * b + h + 1)
                part = st_x2[:, GROUPS * half:GROUPS * (half + 1), :, :].rearrange("p e h w -> p (e h w)")
                copy(st_n[:, half, :], part, func=ACT.Square).then_inc(sq_done, 1)
                copy(st_v[:, 0, half, :], part, scale=X_SCALE).then_inc(v_high, 1)

            def norms(b, h):
                for p in range(2):
                    act.wait_ge(n2_ready, 16 * b + 2 * h + p + 1)
                    if p == 0:
                        act.wait_ge(unit_vec, START + 8 * b + h)
                    copy(st_a[:, p * PIECE:(p + 1) * PIECE], stat_ps[:, 0:PIECE], func=ACT.Abs_reciprocal_sqrt,
                         bias=tiny[:, :])
                    copy(st_n[:, h % 2, p * PIECE:(p + 1) * PIECE], stat_ps[:, 0:PIECE]).then_inc(n2_kept, 1)

            def unit_highs(b, h):
                act.wait_ge(unit_vec, START + 8 * b + h + 1)
                copy(st_hl[:, 0, h % 2, :], st_b[:, :]).then_inc(unit_high, 1)

            def vals_out(b, u, part):
                act.wait_ge(vt_ready, 16 * b + 2 * u + part + 1)
                act.wait_ge(group_done, START + 4 * (8 * b + u))
                copy(vals[:, 16 * part:16 * part + 16, :].rearrange("p n c -> p (n c)"), vals_ps[0:KN, :]).then_inc(vals_done, 1)

            def iteration(i, conv, ls):
                b = i - 1
                if conv:
                    split_high(i, NP - 1)
                    split_low(i, NP - 1)
                    ll_highs(i, 0)
                    ll_highs(i, 1)
                    ll_highs(i, 2)
                if ls:
                    root(gn2, gn2_var, gn2_root, b)
                    half_in(b, 0)
                    half_in(b, 1)
                if conv:
                    act.wait_ge(conv_ready, 11 * i + 1)
                    if not first(i):
                        act.wait_ge(z2_saved, 16 * i)
                    copy(z2[:, :], conv_ps[1][:, 0:H2 * H2], scale=unscale[2]).then_inc(z2_done, 1)
                if ls:
                    norms(b, 0)
                    unit_highs(b, 0)
                    norms(b, 1)
                if conv:
                    act.wait_ge(up2_in, 64 * i + 64)
                    if not first(i):
                        act.wait_ge(z1_saved, 16 * i)
                    for q in range(Q):
                        last = copy(z1[:, q // 2:H1:2, q % 2:H1:2],
                                    up[:, 0, q * H2 * H2:(q + 1) * H2 * H2].rearrange("p (h w) -> p h w", w=H2), scale=0.5)
                    last.then_inc(u2_done, 1)
                if ls:
                    unit_highs(b, 1)
                    half_in(b, 2)
                for j in range(CONV_TILES):
                    if ls:
                        vals_out(b, j, 0)
                    if conv and j == 1:
                        root(gn1, gn1_var, gn1_root, i + 1)
                    if ls and j + 2 < 2 * BANDS:
                        norms(b, j + 2)
                    if conv and j in (3, 5, 7):
                        split_high(i + 1, j // 2 - 1)
                    if ls:
                        vals_out(b, j, 1)
                        if j + 2 < 2 * BANDS:
                            unit_highs(b, j + 2)
                        if j + 3 < 2 * BANDS:
                            half_in(b, j + 3)
                    if conv and j in (3, 5, 7):
                        split_low(i + 1, j // 2 - 1)
                    if conv and j == 7:
                        split_high(i + 1, 3)
                        split_low(i + 1, 3)

            for n in range(3):
                for t in range(0, TAPS, 4):
                    m = min(4, TAPS - t)
                    k = 7 * n + t // 4
                    act.wait_ge(wmixed, k + 1)
                    if n > 0 and t == 0:
                        act.wait_ge(wfull, 7 * n)
                    copy(wmix[:, t * P:(t + m) * P], conv_ps[k % 2][:, 0:m * P]).then_inc(wmix_kept, 1)
                act.wait_ge(wlevel, 3 * n + 3)
                for t in range(0, TAPS, 4):
                    m = min(4, TAPS - t)
                    k = 7 * n + t // 4
                    act.wait_ge(wfull, k + 1)
                    copy(wconv[:, n, 0, t:t + m, :].rearrange("p t o -> p (t o)"), gram_ps[k % 2][:, 0:m * P],
                         scale=wscale[n]).then_inc(whigh, 1)

            act.wait_ge(const_in, 16 * 7)
            root(gn1, gn1_var, gn1_root, 0)
            for k in range(NP - 1):
                split_high(0, k)
                split_low(0, k)
            iteration(0, True, False)
            with act.Fori(1, B) as i:
                iteration(i, True, True)
            iteration(B, False, True)

        @block.vector
        def _(dve):
            V = nc.vector
            steps = Chain(setup, 200)
            for done in (unit_out, unit_vec, flag_done, wgt_done, pad_zero, unit_low):
                dve.sem_inc(done, START)
            V.memset(vals_ps[:, :], 0.0)
            V.memset(guard_ps[:, :], 0.0)

            gn1_chain, gn2_chain = Chain(gn1_link, GN_LINKS), Chain(gn2_link, GN_LINKS)
            prep_chain = Chain(prep_link, 8 * PREP_LINKS)

            def raw_stats(n, c):
                s = c % 2
                dve.wait_ge(raw_in[s], 64 * (4 * n + 1 + c // 2))
                for k in range(2):
                    last = V.bn_stats(bn1[:, 2 * c + k, :], ring[:, s, k * 2 * BANK:(k + 1) * 2 * BANK:2])
                last.then_inc(bn1_done, 1)

            def gn_open(g, bn, bn_done, part, n, per):
                dve.wait_ge(bn_done, per * n + per)
                alone(dve)
                V.bn_aggr(g[:, 0:2], bn[:, :, :].rearrange("p n s -> p (n s)")).then_inc(part, 1)

            def gn_mean(g, chain, part, mm, n):
                chain.round(n)
                dve.wait_ge(mm, 2 * n + 1)
                chain.link(dve, V.tensor_copy(g[:, 2:3], stat_ps[:, 0:1]))
                chain.link(dve, V.tensor_tensor(g[:, 3:4], g[:, 0:1], g[:, 2:3], ALU.subtract))
                V.scalar_tensor_tensor(out=g[:, 3:4], in0=g[:, 3:4], scalar=g[:, 3:4], in1=g[:, 1:2],
                                       op0=ALU.mult, op1=ALU.add).then_inc(part, 1)

            def gn_spread(g, mm, var, n):
                dve.wait_ge(mm, 2 * n + 2)
                V.tensor_scalar(g[:, 4:5], stat_ps[:, 1:2], EPS_GN, None, ALU.add).then_inc(var, 1)

            def gn_close(g, chain, root_done, done, n, scale):
                dve.wait_ge(root_done, n + 1)
                chain.link(dve, V.tensor_scalar(g[:, 6:7], g[:, 4:5], g[:, 5:6], g[:, 5:6], ALU.mult, ALU.mult))
                chain.link(dve, V.tensor_scalar(g[:, 7:8], g[:, 6:7], -0.5, 1.5, ALU.mult, ALU.add))
                chain.link(dve, V.tensor_scalar(g[:, 8:9], g[:, 5:6], g[:, 7:8], scale, ALU.mult, ALU.mult))
                V.tensor_scalar(g[:, 9:10], g[:, 2:3], g[:, 8:9], -1.0, ALU.mult, ALU.mult).then_inc(done, 1)

            def split_rest(n, k):
                dve.wait_ge(high_done, NP * n + k + 1)
                dve.wait_ge(acc_done, NP * n + k + 1)
                V.scalar_tensor_tensor(out=raw_part(k), in0=raw_part(k), scalar=gn1[:, 8:9],
                                       in1=xh[:, PARTS[k][0]:PARTS[k][1], :].rearrange("p h w -> p (h w)"),
                                       op0=ALU.mult, op1=ALU.subtract).then_inc(rest_done, 1)

            def ll_lows(i, k):
                dve.wait_ge(ll_high, 3 * i + k + 1)
                if k < 2:
                    flat = [t[:, 16 * k:16 * k + 16, :].rearrange("p h w -> p (h w)") for t in (xl1, xh1)]
                    V.tensor_tensor(flat[0], conv_ps[k][:, :], flat[1], ALU.subtract).then_inc(ll_low, 1)
                else:
                    flat = [t[:, :, :].rearrange("p h w -> p (h w)") for t in (xl2, xh2)]
                    V.tensor_tensor(flat[0], conv_ps[0][:, 0:H2 * H2], flat[1], ALU.subtract).then_inc(ll_low, 1)

            def level1_out(i, k):
                if k == 0:
                    dve.wait_ge(u2_done, i + 1)
                dve.wait_ge(conv_ready, 11 * i + 2 + k)
                part = z1[:, 16 * k:16 * k + 16, :].rearrange("p h w -> p (h w)")
                V.scalar_tensor_tensor(out=part, in0=conv_ps[k][:, :], scalar=unscale[1], in1=part,
                                       op0=ALU.mult, op1=ALU.add).then_inc(z1_done, 1)

            def add_up(i, q):
                if q == 0:
                    dve.wait_ge(acc_done, NP * i + NP)
                dve.wait_ge(up_in[q % 2], 64 * (2 * i + 1 + q // 2))
                dst = xacc[:, q // 2:H0:2, q % 2:H0:2]
                V.scalar_tensor_tensor(out=dst, in0=up[:, q % 2, :].rearrange("p (h w) -> p h w", w=H1), scalar=0.5,
                                       in1=dst, op0=ALU.mult, op1=ALU.add).then_inc(up_added, 1)

            def x1_out(i, j):
                dve.wait_ge(conv_ready, 11 * i + 4 + j)
                if j == 0:
                    dve.wait_ge(up_added, 4 * i + 4)
                    for saved in x1_saved if not first(i) else ():
                        dve.wait_ge(saved, 16 * i)
                band = (0, 1, 1, 2, 2, 3, 3, 3)[j]
                if not first(i):
                    dve.wait_ge(x2_done, 8 * (i - 1) + 2 * band + 2)
                flat = [t[:, CROWS * j:CROWS * (j + 1), :].rearrange("p h w -> p (h w)") for t in (x1, xacc)]
                V.scalar_tensor_tensor(out=flat[0], in0=conv_ps[j % 2][:, :], scalar=unscale[0], in1=flat[1],
                                       op0=ALU.mult, op1=ALU.add).then_inc(x1_done, 1)
                dve.wait_ge(x1_done, 8 * i + j + 1)
                V.bn_stats(bn2[:, j, :], flat[0]).then_inc(bn2_done, 1)

            def units_open(b, h):
                ch = prep_chain
                if h == 0:
                    ch.round(b)
                dve.wait_ge(n2_kept, START + 16 * b + 2 * h + 2)
                dve.wait_ge(unit_low, START + 8 * b + h)
                ch.link(dve, V.tensor_tensor(st_b[:, :], st_a[:, :], st_a[:, :], ALU.mult))
                ch.link(dve, V.scalar_tensor_tensor(out=st_b[:, :], in0=st_b[:, :], scalar=-0.5, in1=st_n[:, h % 2, :],
                                                    op0=ALU.mult, op1=ALU.mult))

            def units_refine(h):
                sq = st_n[:, h % 2, :]
                prep_chain.link(dve, V.scalar_tensor_tensor(out=st_a[:, :], in0=st_b[:, :], scalar=1.5, in1=st_a[:, :],
                                                            op0=ALU.add, op1=ALU.mult))
                prep_chain.link(dve, V.scalar_tensor_tensor(out=sq, in0=sq, scalar=EPS_SIM ** -0.5, in1=st_a[:, :],
                                                            op0=ALU.mult, op1=ALU.mult))

            def strips_of(h):
                return st_x2[:, GROUPS * (h % 2):GROUPS * (h % 2 + 1), :, :].rearrange("p e h w -> p (e h w)")

            def units_close(b, h):
                prep_chain.link(dve, V.tensor_scalar(st_b[:, :], st_n[:, h % 2, :], 1.0001, None, ALU.is_lt, ALU.add,
                                                     accum_out=short[:, h % 2:h % 2 + 1]))
                V.scalar_tensor_tensor(out=st_b[:, :], in0=strips_of(h), scalar=SIM_SCALE, in1=st_a[:, :],
                                       op0=ALU.mult, op1=ALU.mult).then_inc(unit_vec, 1)

            def value_lows(b, h):
                dve.wait_ge(v_high, 8 * b + h + 1)
                V.scalar_tensor_tensor(out=st_v[:, 1, h % 2, :], in0=strips_of(h), scalar=X_SCALE, in1=st_v[:, 0, h % 2, :],
                                       op0=ALU.mult, op1=ALU.subtract).then_inc(value_low, 1)

            def unit_lows(b, h):
                dve.wait_ge(unit_high, 8 * b + h + 1)
                dve.wait_ge(value_low, 8 * b + h + 1)
                V.tensor_tensor(st_hl[:, 1, h % 2, :], st_b[:, :], st_hl[:, 0, h % 2, :], ALU.subtract).then_inc(unit_low, 1)

            def pad_row(b, h):
                dve.wait_ge(unit_low, START + 8 * b + (6 + h if h < 2 else h - 2) + 1)
                row = 0 if h < 2 else SH - 1
                V.memset(st_x2[:, GROUPS * (h % 2):GROUPS * (h % 2 + 1), row, :], 0.0).then_inc(pad_zero, 1)

            def set_flag(b, h):
                dve.wait_ge(count_ready, 8 * b + h + 1)
                pads = PAD_EDGE if h // 2 in (0, BANDS - 1) else PAD_INNER
                V.tensor_scalar(flag[:, h % 2:h % 2 + 1], stat_ps[0:1, 0:1], float(-pads), None, ALU.add)\
                    .then_inc(flag_done, 1)

            def weights(b, u, k, short_ones):
                n, e = 8 * (8 * b + u) + k, k // 2
                dve.wait_ge(gram_ready, n + 1)
                if k % 2 == 0:
                    dve.wait_ge(group_done, START + 4 * (8 * b + u) + e - 1 if (u > 0 or e > 0) else START + 32 * b)
                alone(dve)
                g = gram_ps[k % 2][0:KN, :].rearrange("p (t n) -> p t n", t=2)
                dst = wgt[:, e % 2, 2 * (k % 2):2 * (k % 2) + 2, :]
                with dve.If(short_ones > 0):
                    V.tensor_scalar(dst, guard_ps[0:KN, :].rearrange("p (t n) -> p t n", t=2), 1.0, None, ALU.min)
                    dve.drain()
                    V.tensor_tensor(g, g, dst, ALU.mult)
                    dve.drain()
                V.scalar_tensor_tensor(
                    out=dst, in0=g, scalar=SIM_SCALE ** 2,
                    in1=tapw[:, :].unsqueeze(1).to_broadcast([KN, 2, 2 * QN]), op0=ALU.add, op1=ALU.mult).then_inc(wgt_done, 1)

            def result(b, u):
                r, half = u // 2, u % 2
                dve.wait_ge(group_done, START + 4 * (8 * b + u + 1))
                if half == 0:
                    dve.wait_ge(x1_res_in, 64 * (4 * b + r + 1))
                    dve.wait_ge(stored, START + 64 * (4 * b + r))
                o = out_ps[:, :].rearrange("p (q h w) -> p q h w", q=Q, h=TH)
                for rp in range(2):
                    dst = ostage[:, rp:2 * TH:2, IMG // 2 * half:IMG // 2 * (half + 1)].rearrange("p h (w c) -> p c h w", c=2)
                    ins = V.tensor_tensor(dst, o[:, 2 * rp:2 * rp + 2], x1_res[:, 2 * rp:2 * rp + 2, :, UW * half:UW * (half + 1)],
                                          ALU.add)
                ins.then_inc(unit_out, 1)

            def tap_weights():
                dve.wait_ge(const_in, 16 * 7)
                dve.wait_ge(taps_in, 16)
                steps.link(dve, V.memset(tapw[:, :], 0.0))
                for t in range(TAPS):
                    steps.link(dve, V.scalar_tensor_tensor(
                        out=tapw[:, :], in0=tap_c[:, t * 2 * QN:(t + 1) * 2 * QN], scalar=spat[0:KN, t:t + 1],
                        in1=tapw[:, :], op0=ALU.mult, op1=ALU.add))
                V.tensor_scalar(tapw[:, :], tapw[:, :], 0.5 / SIM_SCALE ** 2, None, ALU.mult).then_inc(tapw_done, 1)
                dve.wait_ge(tapw_done, 1)

            def iteration(i, conv, ls):
                b = i - 1
                if conv:
                    split_rest(i, NP - 1)
                if ls:
                    gn_open(gn2, bn2, bn2_done, gn2_part, b, 8)
                if conv:
                    ll_lows(i, 0)
                    ll_lows(i, 1)
                if ls:
                    gn_mean(gn2, gn2_chain, gn2_part, gn2_mm, b)
                if conv:
                    ll_lows(i, 2)
                if ls:
                    gn_spread(gn2, gn2_mm, gn2_var, b)
                    gn_close(gn2, gn2_chain, gn2_root, gn2_done, b, 1.0)
                if conv:
                    raw_stats(i + 1, 0)
                    raw_stats(i + 1, 1)
                if ls:
                    for h in range(2):
                        units_open(b, h)
                        units_refine(h)
                        units_close(b, h)
                        value_lows(b, h)
                        unit_lows(b, h)
                        if conv and h == 0:
                            raw_stats(i + 1, 2)
                if conv:
                    level1_out(i, 0)
                    if not ls:
                        raw_stats(i + 1, 2)
                if ls:
                    set_flag(b, 0)
                if conv:
                    level1_out(i, 1)
                    raw_stats(i + 1, 3)
                    gn_open(gn1, bn1, bn1_done, gn1_part, i + 1, 4)
                short_ones = None
                for j in range(CONV_TILES):
                    h = j + 2
                    if ls:
                        dve.wait_ge(flag_done, START + 8 * b + j + 1)
                        alone(dve)
                        short_ones = dve.value_load(flag[0:1, j % 2:j % 2 + 1], min_val=0, max_val=P * UN)
                    for k in range(PAIRS):
                        if ls:
                            if k == 0 and j == 0:
                                set_flag(b, 1)
                            weights(b, j, k, short_ones)
                            if k == 0 and j in (3, 4, 5, 6):
                                pad_row(b, (6, 7, 0, 1)[j - 3])
                            if k == 1 and j > 0:
                                result(b, j - 1)
                            if h < 2 * BANDS:
                                if k == 2:
                                    value_lows(b, h)
                                if k == 3:
                                    units_open(b, h)
                                if k == 4:
                                    units_refine(h)
                                if k == 5:
                                    units_close(b, h)
                                if k == 7:
                                    unit_lows(b, h)
                                    set_flag(b, h)
                        if conv:
                            if k == 6 and j == 0:
                                gn_spread(gn1, gn1_mm, gn1_var, i + 1)
                            if j == 0 and k >= 5:
                                add_up(i, k - 5)
                            if j == 1 and k == 0:
                                add_up(i, 3)
                            if k == 2 and j > 0:
                                x1_out(i, j - 1)
                            if k == 4 and j == 0:
                                gn_mean(gn1, gn1_chain, gn1_part, gn1_mm, i + 1)
                            if k == 3 and j == 1:
                                gn_close(gn1, gn1_chain, gn1_root, gn1_done, i + 1, X_SCALE)
                            if (j, k) in ((3, 7), (5, 7), (7, 4), (7, 7)):
                                split_rest(i + 1, ((3, 7), (5, 7), (7, 4), (7, 7)).index((j, k)))
                    if first(i) and j == 1:
                        tap_weights()
                if conv:
                    x1_out(i, CONV_TILES - 1)
                if ls:
                    result(b, CONV_TILES - 1)

            def peak(n):
                a = gn2[:, 3 * n:3 * n + 3]
                dve.wait_ge(wraw_in[n], 16)
                V.tensor_reduce(out=a[:, 0:1], in_=wraw[n], op=ALU.max, axis=AX_X)
                steps.link(dve, V.tensor_reduce(out=a[:, 1:2], in_=wraw[n], op=ALU.min, axis=AX_X))
                steps.link(dve, V.tensor_scalar(a[:, 1:2], a[:, 1:2], -1.0, 1e-30, ALU.mult, ALU.max))
                V.tensor_tensor(a[:, 2:3], a[:, 0:1], a[:, 1:2], ALU.max).then_inc(wlevel, 1)

            def level_scale(n):
                a = gn2[:, 3 * n:3 * n + 3]
                dve.wait_ge(wlevel_mm, 2 * n + 1)
                V.tensor_reduce(out=a[0:1, 0:1], in_=stat_ps[0:1, 0:P], op=ALU.max, axis=AX_X).then_inc(wlevel, 1)
                dve.wait_ge(wlevel_mm, 2 * n + 2)
                steps.link(dve, V.tensor_copy(a[:, 0:1], stat_ps[:, 0:1]))
                steps.link(dve, V.tensor_scalar(a[:, 1:2].bitcast(I32), a[:, 0:1].bitcast(I32), 0x7F800000, None,
                                                ALU.bitwise_and))
                steps.link(dve, V.reciprocal(a[:, 2:3], a[:, 1:2]))
                V.tensor_scalar(unscale[n], a[:, 1:2], 1 / (W_SCALE * X_SCALE), None, ALU.mult)
                V.tensor_scalar(wscale[n], a[:, 2:3], W_SCALE, None, ALU.mult).then_inc(wlevel, 1)

            peak(0)
            for n in range(3):
                level_scale(n)
                if n < 2:
                    peak(n + 1)
                for t in range(0, TAPS, 4):
                    m = min(4, TAPS - t)
                    k = 7 * n + t // 4
                    dve.wait_ge(whigh, k + 1)
                    V.scalar_tensor_tensor(out=wconv[:, n, 1, t:t + m, :].rearrange("p t o -> p (t o)"),
                                           in0=gram_ps[k % 2][:, 0:m * P], scalar=wscale[n],
                                           in1=wconv[:, n, 0, t:t + m, :].rearrange("p t o -> p (t o)"),
                                           op0=ALU.mult, op1=ALU.subtract).then_inc(wlow, 1)
                if n < 2:
                    raw_stats(0, 2 * n)
                    raw_stats(0, 2 * n + 1)
            gn_open(gn1, bn1, bn1_done, gn1_part, 0, 4)
            gn_mean(gn1, gn1_chain, gn1_part, gn1_mm, 0)
            gn_spread(gn1, gn1_mm, gn1_var, 0)
            gn_close(gn1, gn1_chain, gn1_root, gn1_done, 0, X_SCALE)
            for k in range(NP - 1):
                split_rest(0, k)
            iteration(0, True, False)
            with dve.Fori(1, B) as i:
                iteration(i, True, True)
            iteration(B, False, True)

        @block.tensor
        def _(pe):
            mm = nc.tensor.matmul
            pe.sem_inc(group_done, START)
            def low_pass(dst, high, low, r0, r1, side):
                first = True
                for q in range(Q):
                    for t in (high, low):
                        src = t[:, 2 * r0 + q // 2:2 * r1:2, q % 2:2 * side:2]
                        last = mm(dst, gat_c[:, q, :], src, start=first, stop=(q == Q - 1 and t is low))
                        first = False
                return last

            def conv(level, dst, high, low, r0, nr, side, hook=None):
                taps = sorted(range(TAPS), key=lambda t: t != TAPS // 2)
                n = 0
                for t in taps:
                    dy, dx = t // K - K // 2, t % K - K // 2
                    a0, a1 = max(r0, -dy), min(r0 + nr, side - dy)
                    b0, b1 = max(0, -dx), min(side, side - dx)
                    for w, src in ((0, high), (0, low), (1, high)):
                        if hook:
                            hook(n)
                        last = mm(dst[:, a0 - r0:a1 - r0, b0:b1], wconv[:, level, w, t, :],
                                  src[:, a0 + dy:a1 + dy, b0 + dx:b1 + dx], start=(n == 0), stop=(n == 3 * TAPS - 1))
                        n += 1
                last.then_inc(conv_ready, 1)
                if hook:
                    hook(n)

            def gn_products(g, part, done, n, k):
                pe.wait_ge(part, 2 * n + k + 1)
                mm(stat_ps[:, k:k + 1], average, g[:, 0:1] if k == 0 else g[:, 3:4], start=True, stop=True).then_inc(done, 1)

            def norm_piece(b, h, p):
                pe.wait_ge(sq_done, 8 * b + h + 1)
                pe.wait_ge(n2_kept, START + 16 * b + 2 * h + p)
                pe.wait_ge(flag_done, START + 8 * b + (h if h >= 2 else 0))
                mm(stat_ps[:, 0:PIECE], same_quadrant, st_n[:, h % 2, p * PIECE:(p + 1) * PIECE], start=True, stop=True)\
                    .then_inc(n2_ready, 1)

            def count_short(b, h, gn1_rounds=None):
                pe.wait_ge(unit_vec, START + 8 * b + h + 1)
                pe.wait_ge(n2_kept, START + 16 * b + (4 if h < 2 else 2 * h + 2))
                pe.wait_ge(flag_done, START + 8 * b + h)
                if gn1_rounds is not None:
                    pe.wait_ge(gn1_var, gn1_rounds)
                mm(stat_ps[0:1, 0:1], short[:, h % 2:h % 2 + 1], ones[:, :], start=True, stop=True).then_inc(count_ready, 1)

            def key_values(b, u, part):
                s = u % 2
                pe.wait_ge(unit_in[s], 192 * (4 * b + u // 2 + 1))
                pe.wait_ge(vals_done, START + 16 * b + 2 * u + part)
                alone(pe)
                for e in (2 * part, 2 * part + 1):
                    for g in range(BANDS):
                        for q in range(Q):
                            n, row = ((e % 2) * BANDS + g) * 2 + q // 2, 64 * (q % 2)
                            last = mm(vals_ps[row:row + KQ, C * n:C * n + C],
                                      values[s][0:2 * C, q, e, TH * KW * g:TH * KW * g + KQ], unpair_c[:, :],
                                      start=True, stop=True)
                last.then_inc(vt_ready, 1)

            def gram(b, u, k, short_ones):
                s, e, n = u % 2, k // 2, 8 * (8 * b + u) + k
                pe.wait_ge(wgt_done, START + n - 1 if (u > 0 or k > 1) else START + 64 * b)

                def products(bank, key, query, e_at):
                    for t in range(2):
                        g = 2 * (k % 2) + t
                        window = query[:, :, e_at, :].rearrange("p q (h w) -> p q h w", w=KW)
                        for q in range(Q):
                            row, col = 64 * (q % 2), (2 * t + q // 2) * QN
                            last = mm(bank[row:row + KQ, col:col + QN], key[:, q, e_at, TH * KW * g:TH * KW * g + KQ],
                                      window[:, :, TH * g + 1:TH * g + 1 + TH, 1:1 + TW], start=True, stop=True)
                    return last

                with pe.If(short_ones > 0):
                    pe.wait_ge(wgt_done, START + n)
                    row = 64 + C * (e // 2)
                    norm = norm_rows[s][row:row + 1]
                    products(guard_ps, norm, norm, e % 2)
                last = products(gram_ps[k % 2], keys[s], queries[s], e)
                last.then_inc(gram_ready, 1)

            def filter_group(b, u, e):
                if e == 0:
                    pe.wait_ge(unit_out, START + 8 * b + u)
                pe.wait_ge(vals_done, START + 16 * b + 2 * u + e // 2 + 1)
                pe.wait_ge(wgt_done, START + 8 * (8 * b + u) + 2 * e + 2)
                o = out_ps[:, :].rearrange("p (q h w) -> p q h w", q=Q, h=TH)
                for c in range(2):
                    for g in range(BANDS):
                        last = mm(o[C * g:C * g + C, :, :, TW * e:TW * e + TW], vals[:, (e * BANDS + g) * 2 + c, :],
                                  wgt[:, e % 2, g, c * QN:(c + 1) * QN], start=(c == 0), stop=(c == 1))
                last.then_inc(group_done, 1)

            def iteration(i, conv_on, ls):
                b = i - 1
                short_ones = [None]
                if conv_on:
                    pe.wait_ge(low_done, NP * i + 2)
                    if not first(i):
                        pe.wait_ge(x1_done, 8 * i - 1)
                    ll = [conv_ps[k][:, :].rearrange("p (h w) -> p h w", w=H1) for k in range(2)]
                    low_pass(ll[0], xh, xl, 0, 16, H1).then_inc(ll_ready, 1)
                    cut = PARTS[-1][0] // 2
                    pe.wait_ge(low_done, NP * i + NP - 1)
                    if not first(i):
                        pe.wait_ge(x1_done, 8 * i)
                    low_pass(ll[1][:, 0:cut - 16], xh, xl, 16, cut, H1)
                    pe.wait_ge(low_done, NP * i + NP)
                    low_pass(ll[1][:, cut - 16:16], xh, xl, cut, 32, H1).then_inc(ll_ready, 1)
                if ls:
                    pe.wait_ge(gn1_var, i + 1 if conv_on else B + 1)
                    pe.wait_ge(n2_kept, START + 16 * b)
                    pe.wait_ge(flag_done, START + 8 * b)
                    gn_products(gn2, gn2_part, gn2_mm, b, 0)
                if conv_on:
                    pe.wait_ge(ll_low, 3 * i + 2)
                    t2 = conv_ps[0][:, 0:H2 * H2].rearrange("p (h w) -> p h w", w=H2)
                    low_pass(t2, xh1, xl1, 0, H2, H2).then_inc(ll_ready, 1)
                if ls:
                    gn_products(gn2, gn2_part, gn2_mm, b, 1)
                if conv_on:
                    pe.wait_ge(ll_low, 3 * i + 3)
                    conv(2, conv_ps[1][:, 0:H2 * H2].rearrange("p (h w) -> p h w", w=H2), xh2, xl2, 0, H2, H2)

                def hook_1(n):
                    if ls and n in NORMS_AT:
                        k = NORMS_AT.index(n)
                        if k == 0:
                            pe.wait_ge(gn2_var, b + 1)
                        norm_piece(b, k // 2, k % 2)
                    if ls and n in COUNTS_AT:
                        count_short(b, COUNTS_AT.index(n))

                if conv_on:
                    conv(1, ll[0], xh1, xl1, 0, 16, H1, hook_1)
                    pe.wait_ge(z2_done, i + 1)
                    conv(1, ll[1], xh1, xl1, 16, 16, H1, lambda n: hook_1(3 * TAPS + n))
                else:
                    for n in range(6 * TAPS):
                        hook_1(n)

                for j in range(CONV_TILES):
                    def hook(n, j=j):
                        if n not in HOOKS:
                            return
                        k = HOOKS.index(n)
                        if ls:
                            if k == 0:
                                pe.wait_ge(flag_done, START + 8 * b + j + 1)
                                alone(pe)
                                short_ones[0] = pe.value_load(flag[0:1, j % 2:j % 2 + 1], min_val=0, max_val=P * UN)
                                key_values(b, j, 0)
                            if k == 4:
                                key_values(b, j, 1)
                            if k < PAIRS:
                                gram(b, j, k, short_ones[0])
                            if k in (3, 5, 7, 8):
                                filter_group(b, j, (k - 3) // 2 if k < 8 else 3)
                            if j + 2 < 2 * BANDS:
                                if k == 7:
                                    count_short(b, j + 2, i + 2 if conv_on and j == 0 else None)
                                if k in (1, 2):
                                    norm_piece(b, j + 2, k - 1)
                        if conv_on and j == 0 and k in (4, 6):
                            if ls and k == 4:
                                pe.wait_ge(n2_kept, START + 16 * b + 6)
                            gn_products(gn1, gn1_part, gn1_mm, i + 1, k // 5)

                    if conv_on:
                        if j < 2:
                            pe.wait_ge(z1_done, 2 * i + 1 + j)
                        else:
                            pe.wait_ge(x1_done, 8 * i + j - 1)
                        conv(0, conv_ps[j % 2][:, :].rearrange("p (h w) -> p h w", w=H0), xh, xl, CROWS * j, CROWS, H0, hook)
                    else:
                        for n in range(3 * TAPS + 1):
                            hook(n)

            pe.wait_ge(square_in, 16)
            pe.wait_ge(zeroed, 3)
            for n in range(3):
                w = wraw[n].rearrange("o (i t) -> o t i", t=TAPS)
                pe.wait_ge(wraw_in[n], 16)
                for t in range(0, TAPS, 4):
                    k = 7 * n + t // 4
                    if k >= 2:
                        pe.wait_ge(wmix_kept, k - 1)
                    for s in range(t, min(t + 4, TAPS)):
                        last = mm(conv_ps[k % 2][:, (s - t) * P:(s - t + 1) * P], w[:, s, :], mix, start=True, stop=True)
                    last.then_inc(wmixed, 1)
                pe.wait_ge(wlevel, 3 * n + 1)
                nc.tensor.transpose(stat_ps[0:1, 0:P], gn2[:, 3 * n + 2:3 * n + 3], ident).then_inc(wlevel_mm, 1)
                pe.wait_ge(wlevel, 3 * n + 2)
                for g in range(4):
                    last = mm(stat_ps[C * g:C * g + C, 0:1], ones_row, gn2[0:1, 3 * n:3 * n + 1], start=True, stop=True)
                last.then_inc(wlevel_mm, 1)
                pe.wait_ge(wmix_kept, 7 * n + 7)
                for t in range(0, TAPS, 4):
                    k = 7 * n + t // 4
                    m = min(4, TAPS - t)
                    if k >= 2:
                        pe.wait_ge(wlow, k - 1)
                    mm(gram_ps[k % 2][:, 0:m * P], mix, wmix[:, t * P:(t + m) * P], start=True, stop=True).then_inc(wfull, 1)
            gn_products(gn1, gn1_part, gn1_mm, 0, 0)
            gn_products(gn1, gn1_part, gn1_mm, 0, 1)

            iteration(0, True, False)
            with pe.Fori(1, B) as i:
                iteration(i, True, True)
            iteration(B, False, True)


def const_arrays():
    return dict(zip(("square", "gather", "taps", "unpair"), host_constants()))


_INS = ["x", "L0_conv_w0", "L0_conv_w1", "L0_conv_w2", "L0_conv_bias", "L1_conv_spatial_weight"]


def kernel(**inputs):
    import concourse.bacc as bacc
    from concourse.bass_utils import run_bass_kernel_spmd as run

    nc = bacc.Bacc("TRN2", target_bir_lowering=False, num_devices=1)
    arrays = {n: np.ascontiguousarray(inputs[n]) for n in _INS} | const_arrays()
    args = [nc.dram_tensor(f"in_{n}", a.shape, mybir.dt.from_np(a.dtype), kind="ExternalInput").ap() for n, a in arrays.items()]
    args.append(nc.dram_tensor("out_0", inputs["x"].shape, F32, kind="ExternalOutput").ap())
    build(nc, *args)
    r = run(nc, [{f"in_{n}": a for n, a in arrays.items()}], core_ids=[0])
    return r.results[0]["out_0"]
```
